# Optimizing a Trainium2 kernel written in Bass

```python
import numpy as np
import jax
import jax.numpy as jnp

def _softmax(x, axis=-1):
    return jax.nn.softmax(x, axis=axis)

def _gelu(x):
    return jax.nn.gelu(x, approximate=True)

def _silu(x):
    return jax.nn.silu(x)

def _sigmoid(x):
    return jax.nn.sigmoid(x)

def _layernorm(x, axis=-1, eps=1e-05):
    m = jnp.mean(x, axis=axis, keepdims=True)
    v = jnp.var(x, axis=axis, keepdims=True)
    return (x - m) / jnp.sqrt(v + eps)

def _scatter_add(tgt, idx, src, axis=0):
    return tgt.at[idx].add(src)

def _segment_sum(src, seg, n):
    return jax.ops.segment_sum(src, seg, n)
kernel_name = 'mk_gnn_preln_d1_gnn_r32_8099e9'

def setup_inputs(seed: int=0):
    np.random.seed(seed)
    _w = jnp.asarray

    def _rec_inputs():
        import jax
        import jax.numpy as jnp
        _gk = jax.random.key(seed)
        x = -0.000202 + 1 * jax.random.normal(jax.random.fold_in(_gk, 1), (50000, 128), jnp.float32)
        src = jax.random.randint(jax.random.fold_in(_gk, 2), (50000,), 0, 50000, jnp.int32)
        dst = jnp.minimum((50000 * jax.random.uniform(jax.random.fold_in(_gk, 3), (50000,)) ** 2.0).astype(jnp.int32), 49999)
        _o = jnp.argsort(dst, stable=True)
        src = src[_o]
        dst = dst[_o]
        edge_attr_128 = -2.25437e-05 + 0.999858 * jax.random.normal(jax.random.fold_in(_gk, 11), (50000, 128), jnp.float32)
        edge_type_8 = jax.random.randint(jax.random.fold_in(_gk, 13), (50000,), 0, 8, jnp.int32)
        return (x, src, dst, edge_attr_128, edge_type_8)
    x, src, dst, edge_attr_128, edge_type_8 = _rec_inputs()

    def _L0_gnn_setup():
        import jax, jax.numpy as jnp
        import numpy as np
        N_NODES = 50000
        N_EDGES = 15625
        D = 128
        R = 8
        L = 2
        BN_EPS = 1e-05

        def _rgcn_edge_conv(h, xe, src, dst, etype, w, rt, b):
            m = jax.nn.relu(h[src] + xe)
            n = h.shape[0]
            seg = etype * n + dst
            sums = jax.ops.segment_sum(m, seg, num_segments=R * n)
            cnt = jax.ops.segment_sum(jnp.ones((m.shape[0],), m.dtype), seg, num_segments=R * n)
            mean = sums / jnp.maximum(cnt, 1.0)[:, None]
            hr = mean.reshape(R, n, -1)
            out = jnp.einsum('rnd,rdo->no', hr, w)
            out = out + h @ rt + b
            return out

        def _batch_norm(h, gamma, beta):
            mu = h.mean(axis=0)
            var = jnp.mean((h - mu) ** 2, axis=0)
            return (h - mu) * jax.lax.rsqrt(var + BN_EPS) * gamma + beta
        key = jax.random.key(seed)
        ks = jax.random.split(key, 8)
        x = jax.random.normal(ks[0], (N_NODES, D), dtype=jnp.float32)
        xe = jax.random.normal(ks[1], (N_EDGES, D), dtype=jnp.float32)
        edge_index = jax.random.randint(ks[2], (2, N_EDGES), 0, N_NODES, dtype=jnp.int64)
        edge_type = jax.random.randint(ks[3], (N_EDGES,), 0, R, dtype=jnp.int64)
        w_scale = jnp.sqrt(6.0 / (D + D))
        weight = jax.random.uniform(ks[4], (L, R, D, D), jnp.float32, -w_scale, w_scale)
        root = jax.random.uniform(ks[5], (L, D, D), jnp.float32, -w_scale, w_scale)
        bias = jnp.zeros((L, D), jnp.float32)
        bn_gamma = jnp.ones((L, D), jnp.float32)
        bn_beta = jnp.zeros((L, D), jnp.float32)
        return {'x': x, 'xe': xe, 'edge_index': edge_index, 'edge_type': edge_type, 'weight': weight, 'root': root, 'bias': bias, 'bn_gamma': bn_gamma, 'bn_beta': bn_beta}
    _L0_gnn_all = _L0_gnn_setup()
    _L0_gnn_in = {k: v for k, v in _L0_gnn_all.items() if k in ('weight', 'root', 'bias', 'bn_gamma', 'bn_beta')}
    del _L0_gnn_all
    return {'x': x, 'src': src, 'dst': dst, 'edge_attr_128': edge_attr_128, 'edge_type_8': edge_type_8, 'L0_gnn_weight': _L0_gnn_in['weight'], 'L0_gnn_root': _L0_gnn_in['root'], 'L0_gnn_bias': _L0_gnn_in['bias'], 'L0_gnn_bn_gamma': _L0_gnn_in['bn_gamma'], 'L0_gnn_bn_beta': _L0_gnn_in['bn_beta']}

def reference(x, src, dst, edge_attr_128, edge_type_8, L0_gnn_weight, L0_gnn_root, L0_gnn_bias, L0_gnn_bn_gamma, L0_gnn_bn_beta):
    import jax
    import jax.numpy as jnp

    def _L0_gnn_ref(x, xe, edge_index, edge_type, weight, root, bias, bn_gamma, bn_beta):
        import jax, jax.numpy as jnp
        import numpy as np
        N_NODES = 50000
        N_EDGES = 15625
        D = 128
        R = 8
        L = 2
        BN_EPS = 1e-05

        def _rgcn_edge_conv(h, xe, src, dst, etype, w, rt, b):
            m = jax.nn.relu(h[src] + xe)
            n = h.shape[0]
            seg = etype * n + dst
            sums = jax.ops.segment_sum(m, seg, num_segments=R * n)
            cnt = jax.ops.segment_sum(jnp.ones((m.shape[0],), m.dtype), seg, num_segments=R * n)
            mean = sums / jnp.maximum(cnt, 1.0)[:, None]
            hr = mean.reshape(R, n, -1)
            out = jnp.einsum('rnd,rdo->no', hr, w)
            out = out + h @ rt + b
            return out

        def _batch_norm(h, gamma, beta):
            mu = h.mean(axis=0)
            var = jnp.mean((h - mu) ** 2, axis=0)
            return (h - mu) * jax.lax.rsqrt(var + BN_EPS) * gamma + beta
        src, dst = (edge_index[0], edge_index[1])
        h = x
        for l in range(L):
            h = _rgcn_edge_conv(h, xe, src, dst, edge_type, weight[l], root[l], bias[l])
            h = _batch_norm(h, bn_gamma[l], bn_beta[l])
            if l != L - 1:
                h = jax.nn.relu(h)
        return h
    edge_index = jnp.stack([src, dst])
    h = jnp.maximum(_layernorm(x, axis=-1), 0.0)
    x = x + _L0_gnn_ref(h, edge_attr_128, edge_index, edge_type_8, L0_gnn_weight, L0_gnn_root, L0_gnn_bias, L0_gnn_bn_gamma, L0_gnn_bn_beta)
    return x

_drawn_inputs = setup_inputs


def setup_inputs(seed=0):
    import zlib

    import numpy as np

    out = dict(_drawn_inputs(seed))
    spreads = {'L0_gnn_bias': (0.0, 0.1), 'L0_gnn_bn_gamma': (1.0, 0.2), 'L0_gnn_bn_beta': (0.0, 0.1)}
    factors = {}
    for name, (base, spread) in spreads.items():
        noise = np.random.default_rng([zlib.crc32(name.encode()), seed]).standard_normal(out[name].shape)
        drawn = base * np.exp(spread * noise) if base else spread * noise
        out[name] = jnp.asarray(drawn.astype(out[name].dtype))
    for name, factor in factors.items():
        out[name] = (out[name] * factor).astype(out[name].dtype)
    return out
```

```python
import concourse.bass as bass
from concourse import mybir
from contextlib import ExitStack

P = 128
FP32 = mybir.dt.float32
I32 = mybir.dt.int32
U32 = mybir.dt.uint32
ALU = mybir.AluOpType
ACT = mybir.ActivationFunctionType
BN_EPS = 1e-5
LN_EPS = 1e-5


def divisor_up_to(n, most):
    return max(k for k in range(1, most + 1) if n % k == 0)


def wait(eng, sem, value):
    if isinstance(value, int) and value <= 0:
        return
    eng.wait_ge(sem, value)


class Chain:

    def __init__(self, eng, sem):
        self.eng, self.sem, self.count = eng, sem, 0

    def mark(self, instruction):
        instruction.then_inc(self.sem, 1)
        self.count = self.count + 1

    def link(self, instruction):
        self.mark(instruction)
        self.eng.wait_ge(self.sem, self.count)


def pair_loop(eng, pairs, body, chain=None):
    if not pairs:
        return
    before = chain.count if chain else 0
    body(0)
    step = chain.count - before if chain else 0
    if pairs > 1:
        with eng.Fori(1, pairs) as i:
            if chain:
                chain.count = i * step + before
            body(i)
        if chain:
            chain.count = before + step * pairs


def gnn_kernel(nc, x, src, dst, edge_attr, edge_type, weight, root, bias, gamma, beta, out):
    N, D = x.shape
    E = src.shape[0]
    L, R = weight.shape[0], weight.shape[1]
    assert D == P and edge_attr.shape == (E, D) and L == 2

    F = -(-N // P)
    FE = -(-E // P)
    assert F == FE
    CW = divisor_up_to(F, 17)
    NC = F // CW
    PV = N - (P - 1) * F
    assert E == N and 0 < PV <= F
    FULL = PV // CW
    ROWS = P * (F + 2)
    REPEAT = P * F
    PADDST = P * (F + 1)
    G = 8
    H = 4
    NT = -(-((E + R * (P - 1)) // P) // (2 * G)) * 2 * G
    NG = NT // G
    TAIL = NT - E // P
    M = D + 4
    KEYS = (R + 1) * ROWS
    BIG = float(1 << 22)

    def valid(c):
        return max(0, min(CW, PV - c * CW)) if isinstance(c, int) else CW

    def n_dma(c):
        v = valid(c)
        return 1 if v == CW else 3 if v else 2

    def arrived(c, i, s):
        if not isinstance(c, int):
            return i * 16 + 16
        return 16 * sum(n_dma(k) for k in range(s, c + 1, 2))

    def groups_of(cols):
        return [(a, min(H, cols - a)) for a in range(0, cols, H)]

    NGR = len(groups_of(CW))

    ctx = ExitStack()
    with ctx:
        def sb(name, shape, dt=FP32):
            return ctx.enter_context(nc.sbuf_tensor(name, shape, dt))

        def pb(name):
            return ctx.enter_context(nc.psum_tensor(name, [P, H * D], FP32))

        def sem(name):
            return ctx.enter_context(nc.semaphore(name))

        def dram(name, shape):
            return nc.dram_tensor(name, shape, FP32, kind="Internal").ap()

        h_tab = [dram("h0_rows", [P * F, D]), dram("h1_rows", [P * F, D])]
        acc = [[dram(f"acc_{l}_{k}", [ROWS, D]) for k in range(2)] for l in range(L)]
        sorted_rows = dram("sorted_rows", [NT * P, M])
        key_count = dram("key_count", [KEYS + P, 1])
        sum_rows = dram("sum_rows", [P * F, D])

        ident = sb("ident", [P, P])
        ones = sb("ones", [P, P])
        before_p = sb("before_p", [P, P])
        rank_w = sb("rank_w", [P, P])
        pidx = sb("pidx", [P, 1])
        pidx_i = sb("pidx_i", [P, 1], I32)
        zeros = sb("zeros", [P, CW * D])
        tiota_i = sb("tiota_i", [1, NT], I32)
        tiota = sb("tiota", [1, NT])
        w_sb = [sb(f"w_sb{l}", [P, R * D]) for l in range(L)]
        root_sb = sb("root_sb", [P, L * D])
        vec = sb("vec", [P, 6])
        bias_b = sb("bias_b", [P, L, D])
        bn_col = sb("bn_col", [P, L, 2])
        bn_b = sb("bn_b", [P, L, 2, D])

        type_i = sb("type_i", [P, FE], I32)
        src_i = sb("src_i", [P, FE], I32)
        dst_i = sb("dst_i", [P, FE], I32)
        type_f = sb("type_f", [P, FE])
        dst_f = sb("dst_f", [P, FE])
        key = sb("key", [P, FE])
        key_i = sb("key_i", [P, FE], U32)
        add_i = sb("add_i", [P, FE], U32)
        in_tile = sb("in_tile", [P, FE])
        total = sb("total", [P, FE])
        inv = sb("inv", [P, FE])
        pos = sb("pos", [P, FE])
        pos_i = sb("pos_i", [P, FE], U32)
        cum = sb("cum", [P, R, FE])
        eq = sb("eq", [P, FE])
        tmp = sb("tmp", [P, FE])
        zcol = sb("zcol", [P, FE])
        tot = sb("tot", [P, R])
        off = sb("off", [P, R])
        grand = sb("grand", [P, R])
        ntile = sb("ntile", [P, R])
        ntile_i = sb("ntile_i", [P, R], I32)
        ends = sb("ends", [P, R])
        base = sb("base", [P, R])
        padn = sb("padn", [P, R])
        padpos = sb("padpos", [P, R + TAIL])
        padpos_i = sb("padpos_i", [P, R + TAIL], U32)
        padrow = sb("padrow", [P, M])
        tile_type = sb("tile_type", [1, NT])
        tile_type_i = sb("tile_type_i", [1, NT], I32)
        scat_idx = sb("scat_idx", [P, NT], U32)

        key_st = sb("key_st", [P, 2, CW])
        same = sb("same", [P, 2, D])
        junk = sb("junk", [P, D])
        val_st = sb("val_st", [P, 2, CW])
        cnt_idx = sb("cnt_idx", [P, 2, CW], U32)
        cnt_val = sb("cnt_val", [P, 2, CW])
        meta = sb("meta", [P, 2, CW, M])
        pos_st = sb("pos_st", [P, 2, CW], U32)
        xc = sb("xc", [P, 2, CW, D])
        yc = sb("yc", [P, 2, CW, D])
        oc = sb("oc", [P, 2, CW, D])
        st6 = sb("st6", [P, CW, 6])
        mv = sb("mv", [P, CW, 2])
        ve = sb("ve", [P, CW])
        sd = sb("sd", [P, CW])
        rstd = sb("rstd", [P, 2, CW])
        nmr = sb("nmr", [P, 2, CW])
        ht = sb("ht", [P, 2, H * D])
        xb = sb("xb", [P, 2, G, M])
        src_st = sb("src_st", [P, 2, G], U32)
        hb = sb("hb", [P, 2, G, D])
        sm = sb("sm", [P, 2, H * D])
        tb = sb("tb", [P, 2, H * D])
        mb = sb("mb", [P, 2, H * D])
        mt = sb("mt", [P, 2, H * D])
        yb = sb("yb", [P, 2, G, D])
        rank_st = sb("rank_st", [P, 2, G])
        first = sb("first", [P, H])
        dsub = sb("dsub", [P, H])
        idx_f = sb("idx_f", [P, H])
        idx_st = sb("idx_st", [P, 2, G], U32)
        NST = NC * NGR + NGR
        bstat = sb("bstat", [P, NST, 6])
        bst = sb("bst", [P, 2, 6])
        bmv = sb("bmv", [P, 2])
        bsd = sb("bsd", [P, 1])
        brs = sb("brs", [P, 1])

        ps_t = [pb("ps_t0"), pb("ps_t1")]
        ps_o = [pb("ps_o0"), pb("ps_o1")]
        ps_m = [pb("ps_m0"), pb("ps_m1")]
        ps_y = [pb("ps_y0"), pb("ps_y1")]

        consts = sem("consts")
        pool_own = sem("pool_own")
        dve_own = sem("dve_own")
        act_own = sem("act_own")
        dve_idle = sem("dve_idle")
        idle = sem("idle")
        params_in = sem("params_in")
        idx_in = sem("idx_in")
        blank = sem("blank")
        tot_ready = sem("tot_ready")
        off_ready = sem("off_ready")
        off_read = sem("off_read")
        bias_ps = sem("bias_ps")
        types_ready = sem("types_ready")
        pos_ready = sem("pos_ready")
        tables_zero = sem("tables_zero")
        kst_ready = sem("kst_ready")
        keyb_ready = sem("keyb_ready")
        keyb_read = sem("keyb_read")
        cidx_ready = sem("cidx_ready")
        chain_sem = sem("chain_sem")
        cnt_got = sem("cnt_got")
        total_ready = sem("total_ready")
        inv_ready = sem("inv_ready")
        attr_in = [sem("attr_in0"), sem("attr_in1")]
        sorted_out = [sem("sorted_out0"), sem("sorted_out1")]
        pads_out = sem("pads_out")
        xc_in = [sem("xc_in0"), sem("xc_in1")]
        ve_ready = sem("ve_ready")
        sd_ready = sem("sd_ready")
        rs_ready = sem("rs_ready")
        h_ready = sem("h_ready")
        h_out = [sem("h_out0"), sem("h_out1")]
        tr_ready = sem("tr_ready")
        ht_ready = sem("ht_ready")
        o_ps = sem("o_ps")
        o_ready = sem("o_ready")
        o_out = [sem("o_out0"), sem("o_out1")]
        xb_in = [sem("xb_in0"), sem("xb_in1")]
        src_ready = sem("src_ready")
        got = [[sem(f"got{s}{q}") for q in range(2)] for s in range(2)]
        d_ready = sem("d_ready")
        s_ready = sem("s_ready")
        t_ready = sem("t_ready")
        m_ready = sem("m_ready")
        ms_ready = sem("ms_ready")
        mt_ready = sem("mt_ready")
        y_ps = sem("y_ps")
        y_ready = sem("y_ready")
        added = [sem("added0"), sem("added1")]
        group_added = sem("group_added")
        ab_in = [sem("ab_in0"), sem("ab_in1")]
        sum_ready = sem("sum_ready")
        sum_out = [sem("sum_out0"), sem("sum_out1")]
        st_ps = sem("st_ps")
        st_read = sem("st_read")
        bn_var = sem("bn_var")
        bn_sd = sem("bn_sd")
        bn_ready = sem("bn_ready")
        bnb_ps = sem("bnb_ps")
        bnb_ready = sem("bnb_ready")
        f_in = [sem("f_in0"), sem("f_in1")]
        f_ready = sem("f_ready")
        f_out = [sem("f_out0"), sem("f_out1")]

        block = ctx.enter_context(nc.Block())

        def by_partition(a, rows):
            return bass.AP(a.tensor, 0, [[F * D, P], [1, rows * D]])

        def row_dma(eng, tile, a, c, semaphore, load):
            v = valid(c)
            if v == CW:
                far = by_partition(a, PV)[:, bass.ds(c * (CW * D), CW * D)].rearrange("p (c d) -> p c d", d=D)
                pieces = [(tile, far)]
            else:
                far = bass.AP(a.tensor, c * CW * D, [[F * D, P - 1], [D, CW], [1, D]])
                pieces = [(tile[0:112], far[0:112]), (tile[112:P - 1], far[112:P - 1])]
                if v:
                    far = bass.AP(a.tensor, (P - 1) * F * D + c * CW * D, [[F * D, 1], [D, v], [1, D]])
                    pieces.append((tile[P - 1:P, 0:v], far))
            for near, far in pieces:
                o, i = (near, far) if load else (far, near)
                eng.dma_start(o, i).then_inc(semaphore, 16)

        def table_dma(eng, tile, a, c, semaphore, load):
            far = by_partition(a, F)[:, bass.ds(c * (CW * D), CW * D)]
            near = tile.rearrange("p c d -> p (c d)")
            o, i = (near, far) if load else (far, near)
            eng.dma_start(o, i).then_inc(semaphore, 16)

        def chunks(eng, body, chain=None):
            pairs = FULL // 2

            def pair(i):
                for s in range(2):
                    body(2 * i + s, i, s)
            pair_loop(eng, pairs, pair, chain)
            for c in range(2 * pairs, NC):
                body(c, c // 2, c % 2)

        def even_chunks(eng, body, chain=None):
            pairs = NC // 2

            def pair(i):
                for s in range(2):
                    body(2 * i + s, i, s)
            pair_loop(eng, pairs, pair, chain)
            for c in range(2 * pairs, NC):
                body(c, c // 2, c % 2)

        def last_count(slot):
            return arrived(NC - 1 - (NC - 1 - slot) % 2, 0, slot)

        def plain_uses(slot):
            return (NC - slot + 1) // 2

        def stat_groups(c):
            gs = groups_of(CW)
            v = valid(c)
            if v in (0, CW):
                return gs
            cut = [(a, w) for a, w in [(0, v)] if w <= H] + [(a + v, w) for a, w in groups_of(CW - v)]
            assert v <= H and len(cut) == NGR
            return cut

        @block.sync
        def _(sp):
            with nc.allow_non_contiguous_dma(reason="one column of parameters, once"):
                for l in range(L):
                    for k, a in enumerate((bias, gamma, beta)):
                        sp.dma_start(vec[:, 3 * l + k:3 * l + k + 1], a[l, :].rearrange("(d u) -> d u", u=1)).then_inc(params_in, 16)
            for l in range(L):
                sp.dma_start(w_sb[l][:, :].rearrange("d (r o) -> d r o", r=R), weight[l].rearrange("r d o -> d r o")).then_inc(params_in, 16)
                sp.dma_start(root_sb[:, l * D:(l + 1) * D], root[l]).then_inc(params_in, 16)
            sp.wait_ge(blank, 1)
            for near, far in ((type_i, edge_type), (src_i, src), (dst_i, dst)):
                for a, b in ((0, 112), (112, P - 1)):
                    sp.dma_start(near[a:b, :], bass.AP(far.tensor, a * FE, [[FE, b - a], [1, FE]])).then_inc(idx_in, 16)
                sp.dma_start(near[P - 1:P, 0:PV], bass.AP(far.tensor, (P - 1) * FE, [[FE, 1], [1, PV]])).then_inc(idx_in, 16)
            sp.wait_ge(blank, 2)
            n = (KEYS + P) // P
            flat = key_count.rearrange("(p c) u -> p (c u)", p=P)
            for a in range(0, n, CW * D):
                b = min(n, a + CW * D)
                sp.dma_start(flat[:, a:b], zeros[:, 0:b - a]).then_inc(tables_zero, 16)
            for l in range(L):
                sp.dma_start(acc[l][0][P * F:ROWS, :].rearrange("(p c) d -> p (c d)", p=P), zeros[:, 0:2 * D]).then_inc(tables_zero, 16)
                sp.dma_start(acc[l][1][P * F:ROWS, :].rearrange("(p c) d -> p (c d)", p=P), zeros[:, 0:2 * D]).then_inc(tables_zero, 16)
                for c in range(NC):
                    table_dma(sp, zeros[:, :].rearrange("p (c d) -> p c d", d=D), acc[l][1], c, tables_zero, False)

            def attrs(c, i, s):
                wait(sp, sorted_out[s], i * (16 * CW))
                row_dma(sp, meta[:, s, :, 0:D], edge_attr, c, attr_in[s], True)
            sp.wait_ge(blank, 3)
            chunks(sp, attrs)

            for l in range(L):
                if l == 0:
                    for s in range(2):
                        sp.wait_ge(sorted_out[s], 16 * CW * plain_uses(s))
                    sp.wait_ge(pads_out, 16 * (R + TAIL))

                def rows(i, l=l):
                    for s in range(2):
                        g = 2 * i + (s + l * NG)
                        wait(sp, m_ready, 2 * g - 2)
                        far = sorted_rows[bass.ds((2 * i + s) * (G * P), G * P), :].rearrange("(g p) c -> p g c", p=P)
                        sp.dma_start(xb[:, s, :, :], far).then_inc(xb_in[s], 16)
                pair_loop(sp, NG // 2, rows)

                for k in range(2):
                    sp.wait_ge(added[k], 16 * (l + 1) * NT // 2)
                if l == 1:
                    sp.wait_ge(o_ready, 2 * NC * NGR)
                    sp.wait_ge(tr_ready, 2 * NC * NGR)

                def ab(c, i, s, l=l):
                    if not isinstance(c, int) or c >= 2:
                        sp.wait_ge(sum_ready, c + (l * NC - 1))
                    table_dma(sp, xc[:, s, :, :], acc[l][0], c, ab_in[s], True)
                    table_dma(sp, yc[:, s, :, :], acc[l][1], c, ab_in[s], True)

                if l == 0:
                    for s in range(2):
                        sp.wait_ge(h_out[s], 16 * plain_uses(s))
                    sp.wait_ge(o_ps, NC * NGR)
                even_chunks(sp, ab)
                if l == 1:
                    break
            for s in range(2):
                sp.wait_ge(sum_out[s], 16 * 2 * plain_uses(s))
            sp.wait_ge(st_ps, 2 * NC * NGR)
            sp.wait_ge(bnb_ready, 2)

            def final(c, i, s):
                wait(sp, f_ready, c - 1)
                table_dma(sp, xc[:, s, :, :], sum_rows, c, f_in[s], True)
                row_dma(sp, yc[:, s, :, :], x, c, f_in[s], True)
            chunks(sp, final)
            for s in range(2):
                sp.wait_ge(f_out[s], last_count(s))

        @block.gpsimd
        def _(pool):
            own = Chain(pool, pool_own)
            gp = nc.gpsimd
            own.link(gp.memset(ident[:, :], 0.0))
            gp.affine_select(out=ident[:, :], in_=ident[:, :], compare_op=ALU.not_equal, fill=1.0, base=0,
                             pattern=[[-1, P]], channel_multiplier=1).then_inc(consts, 1)
            own.link(gp.memset(before_p[:, :], 1.0))
            gp.affine_select(out=before_p[:, :], in_=before_p[:, :], compare_op=ALU.is_gt, fill=0.0, base=0,
                             pattern=[[1, P]], channel_multiplier=-1).then_inc(consts, 1)
            own.link(gp.memset(rank_w[:, :], float(2 * P + 1)))
            gp.affine_select(out=rank_w[:, :], in_=rank_w[:, :], compare_op=ALU.is_gt, fill=1.0, base=0,
                             pattern=[[-1, P]], channel_multiplier=1).then_inc(consts, 1)
            gp.iota(pidx_i[:, :], pattern=[[0, 1]], base=0, channel_multiplier=1).then_inc(consts, 1)
            gp.iota(tiota_i[:, :], pattern=[[1, NT]], base=0, channel_multiplier=0).then_inc(consts, 1)

            def indexed(reg_waits, **kw):
                for s, v in reg_waits:
                    if isinstance(v, int):
                        wait(pool, s, v)
                    else:
                        pool.wait_ge(s, v)
                        pool.sem_inc(idle, 1)
                return pool.indirect_dma_start(**kw)

            def at(ap):
                return bass.IndirectOffsetOnAxis(ap=ap, axis=0)

            pool.wait_ge(cidx_ready, 1)
            n_key = -(-((KEYS + P) // P) // (CW * D))
            pool.wait_ge(tables_zero, 16 * (n_key + L * (2 + NC)))

            def count_chunk(c, i, s):
                own.mark(gp.tensor_copy(cnt_idx[:, s, :], add_i[:, bass.ds(c * CW, CW)]))
                own.link(gp.tensor_copy(cnt_val[:, s, :], in_tile[:, bass.ds(c * CW, CW)]))
                pool.sem_inc(idle, 1)
                for j in range(CW):
                    indexed([(chain_sem, c * (16 * CW) + 16 * j)], out=key_count, out_offset=at(cnt_idx[:, s, j:j + 1]),
                            in_=cnt_val[:, s, j:j + 1], in_offset=None, compute_op=ALU.add).then_inc(chain_sem, 16)
            even_chunks(pool, count_chunk, own)
            pool.wait_ge(chain_sem, 16 * FE)

            def total_chunk(c, i, s):
                own.link(gp.tensor_copy(cnt_idx[:, s, :], key_i[:, bass.ds(c * CW, CW)]))
                pool.sem_inc(idle, 1)
                for j in range(CW):
                    indexed([], out=cnt_val[:, s, j:j + 1], out_offset=None, in_=key_count,
                            in_offset=at(cnt_idx[:, s, j:j + 1])).then_inc(cnt_got, 16)
                pool.wait_ge(cnt_got, c * (16 * CW) + 16 * CW)
                own.link(gp.tensor_copy(total[:, bass.ds(c * CW, CW)], cnt_val[:, s, :]))
            even_chunks(pool, total_chunk, own)
            pool.sem_inc(total_ready, 1)

            pool.wait_ge(pos_ready, 1)
            for j in range(R + TAIL):
                indexed([], out=sorted_rows, out_offset=at(padpos_i[:, j:j + 1]), in_=padrow[:, :], in_offset=None,
                        bounds_check=NT * P - 1, oob_is_err=False).then_inc(pads_out, 16)
            pool.wait_ge(inv_ready, 1)

            def place_chunk(c, i, s):
                wait(pool, sorted_out[s], i * (16 * CW))
                own.mark(gp.tensor_copy(pos_st[:, s, :], pos_i[:, bass.ds(c * CW, CW)]))
                own.mark(gp.tensor_copy(meta[:, s, :, D].bitcast(I32), src_i[:, bass.ds(c * CW, CW)]))
                own.mark(gp.tensor_copy(meta[:, s, :, D + 1], dst_f[:, bass.ds(c * CW, CW)]))
                own.link(gp.tensor_copy(meta[:, s, :, D + 2], inv[:, bass.ds(c * CW, CW)]))
                pool.sem_inc(idle, 1)
                for j in range(CW):
                    waits = [(attr_in[s], arrived(c, i, s))] if j == 0 else []
                    indexed(waits, out=sorted_rows, out_offset=at(pos_st[:, s, j:j + 1]), in_=meta[:, s, j, :],
                            in_offset=None, bounds_check=NT * P - 1, oob_is_err=False).then_inc(sorted_out[s], 16)
            chunks(pool, place_chunk, own)

            for l in range(L):
                first_tile = l * NT

                def gather(g, i, s, j, l=l):
                    waits = []
                    if j == 0:
                        waits.append((xb_in[s], i * 16 + 16))
                    if j % H == 0:
                        waits.append((t_ready, g * 2 + (j // H - 3)))
                    indexed(waits, out=hb[:, s, j, :], out_offset=None, in_=h_tab[l],
                            in_offset=at(xb[:, s, j, D:D + 1].bitcast(U32))).then_inc(got[s][j // H], 16)

                def add(g, s, j, l=l):
                    k = j % 2
                    waits = []
                    if j % H == 0:
                        waits.append((y_ready, g * 2 + (j // H + 1)))
                    waits.append((added[k], (g * (G // 2) + j // 2) * 16))
                    dma = indexed(waits, out=acc[l][k], out_offset=at(idx_st[:, s, j:j + 1]), in_=yb[:, s, j, :],
                                  in_offset=None, compute_op=ALU.add)
                    dma.then_inc(added[k], 16)
                    if j == 1:
                        pool.sem_inc(group_added, 1)

                if l == 0:
                    for s in range(2):
                        pool.wait_ge(h_out[s], 16 * plain_uses(s))
                else:
                    for s in range(2):
                        pool.wait_ge(sum_out[s], 16 * plain_uses(s))
                for j in range(G):
                    gather(l * NG, l * NG // 2, 0, j)
                for s in range(2):
                    pool.wait_ge(o_out[s], 16 * plain_uses(s) * (l + 1))
                g = l * NG
                for j in range(G):
                    gather(g + 1, g // 2, 1, j)
                    add(g, 0, j)

                def pair(i, l=l):
                    g = 2 * i + l * NG
                    for s in range(2):
                        for j in range(G):
                            gather(g + s, i + l * NG // 2, s, j)
                            add(g + (s - 1), 1 - s, j)
                if NG > 2:
                    with pool.Fori(1, NG // 2) as i:
                        pair(i)
                for j in range(G):
                    add(l * NG + NG - 1, 1, j)

        @block.vector
        def _(dve):
            v = nc.vector
            own = Chain(dve, dve_own)
            v.memset(zcol[:, :], 0.0)
            own.link(v.memset(ones[:, :], 1.0))
            v.memset(type_i[:, :], R)
            v.memset(src_i[:, :], 0)
            v.memset(dst_i[:, :], 0).then_inc(blank, 1)
            v.memset(zeros[:, :], 0.0).then_inc(blank, 1)
            v.memset(xc[:, :, :, :], 0.0)
            v.memset(meta[:, :, :, :], 0.0).then_inc(blank, 1)
            own.link(v.memset(padrow[:, :], 0.0))
            v.memset(padrow[:, D + 1:D + 2], float(PADDST))
            dve.wait_ge(consts, 5)
            v.tensor_copy(pidx[:, :], pidx_i[:, :])
            v.tensor_copy(tiota[:, :], tiota_i[:, :])
            dve.wait_ge(idx_in, 9 * 16)
            v.tensor_copy(type_f[:, :], type_i[:, :])
            own.link(v.tensor_copy(dst_f[:, :], dst_i[:, :]))
            own.link(v.scalar_tensor_tensor(key[:, :], type_f[:, :], float(ROWS), dst_f[:, :], ALU.mult, ALU.add))
            own.mark(v.tensor_copy(key_i[:, :], key[:, :]))

            for r in range(R):
                own.link(v.tensor_scalar(eq[:, :], type_f[:, :], float(r), None, ALU.is_equal))
                own.link(v.tensor_tensor_scan(cum[:, r, :], eq[:, :], zcol[:, :], 0.0, ALU.add, ALU.add))
                own.link(v.tensor_copy(tot[:, r:r + 1], cum[:, r, FE - 1:FE]))
            dve.sem_inc(tot_ready, 1)
            dve.wait_ge(off_ready, 1)
            v.tensor_copy(off[:, :], ps_t[0][:, 0:R])
            own.link(v.tensor_copy(grand[:, :], ps_t[0][:, R:2 * R]))
            for l in range(L):
                last = v.tensor_copy(bias_b[:, l, :], ps_t[0][:, (l + 1) * D:(l + 2) * D])
            last.then_inc(off_read, 1)
            own.link(v.tensor_scalar(tmp[:, 0:R], grand[:, :], float(P - 1), None, ALU.add))
            own.link(v.tensor_copy(ntile_i[:, :], tmp[:, 0:R]))
            own.link(v.tensor_scalar(ntile_i[:, :], ntile_i[:, :], P.bit_length() - 1, None, ALU.arith_shift_right))
            own.link(v.tensor_copy(ntile[:, :], ntile_i[:, :]))
            own.link(v.tensor_tensor_scan(ends[:, :], ntile[:, :], zcol[:, 0:R], 0.0, ALU.add, ALU.add))
            own.link(v.tensor_tensor(base[:, :], ends[:, :], ntile[:, :], ALU.subtract))
            own.link(v.tensor_scalar(tile_type[:, :], tiota[:, :], base[0:1, 1:2], None, ALU.is_ge))
            for r in range(2, R):
                own.link(v.scalar_tensor_tensor(tile_type[:, :], tiota[:, :], base[0:1, r:r + 1], tile_type[:, :], ALU.is_ge, ALU.add))
            v.tensor_copy(tile_type_i[:, :], tile_type[:, :]).then_inc(types_ready, 1)
            own.link(v.tensor_scalar(base[:, :], base[:, :], float(P), None, ALU.mult))
            own.link(v.tensor_tensor(padpos[:, 0:R], base[:, :], grand[:, :], ALU.add))
            own.link(v.tensor_scalar(padpos[:, 0:R], padpos[:, 0:R], pidx[:, 0:1], None, ALU.add))
            own.link(v.scalar_tensor_tensor(padn[:, :], ntile[:, :], float(P), grand[:, :], ALU.mult, ALU.subtract))
            own.link(v.tensor_scalar(padn[:, :], padn[:, :], pidx[:, 0:1], BIG, ALU.is_le, ALU.mult))
            own.link(v.tensor_tensor(padpos[:, 0:R], padpos[:, 0:R], padn[:, :], ALU.add))
            own.link(v.tensor_scalar(tmp[:, 0:1], ends[:, R - 1:R], float(P), pidx[:, 0:1], ALU.mult, ALU.add))
            for j in range(TAIL):
                own.mark(v.tensor_scalar(padpos[:, R + j:R + j + 1], tmp[:, 0:1], float(j * P), None, ALU.add))
            dve.wait_ge(dve_own, own.count)
            own.mark(v.tensor_copy(padpos_i[:, :], padpos[:, :]))
            own.link(v.tensor_tensor(off[:, :], off[:, :], base[:, :], ALU.add))
            own.link(v.tensor_scalar(off[:, :], off[:, :], -1.0, None, ALU.add))
            own.link(v.tensor_scalar(pos[:, :], type_f[:, :], float(R), BIG, ALU.is_equal, ALU.mult))
            for r in range(R):
                own.link(v.tensor_scalar(eq[:, :], type_f[:, :], float(r), None, ALU.is_equal))
                own.link(v.scalar_tensor_tensor(tmp[:, :], cum[:, r, :], off[:, r:r + 1], eq[:, :], ALU.add, ALU.mult))
                own.link(v.tensor_tensor(pos[:, :], pos[:, :], tmp[:, :], ALU.add))
            v.tensor_copy(pos_i[:, :], pos[:, :]).then_inc(pos_ready, 1)

            def same_key(c, i, s):
                v.tensor_copy(key_st[:, s, :], key[:, bass.ds(c * CW, CW)]).then_inc(kst_ready, 1)
                for g, (a, w) in enumerate(groups_of(CW)):
                    dve.wait_ge(keyb_ready, c * NGR + (g + 1))
                    for j in range(w):
                        own.link(v.tensor_scalar(same[:, j % 2, :], ps_t[g % 2][:, j * D:(j + 1) * D],
                                                 key_st[:, s, a + j:a + j + 1], None, ALU.is_equal))
                        ins = v.tensor_tensor_reduce(out=junk[:, :], in0=same[:, j % 2, :], in1=rank_w[:, :], scale=1.0,
                                                     scalar=0.0, op0=ALU.mult, op1=ALU.add,
                                                     accum_out=val_st[:, s, a + j:a + j + 1])
                        if j < w - 1:
                            own.link(ins)
                        else:
                            own.link(ins)
                            dve.sem_inc(keyb_read, 1)
                own.link(v.tensor_copy(in_tile[:, bass.ds(c * CW, CW)], val_st[:, s, :]))
            even_chunks(dve, same_key, own)
            own.link(v.tensor_scalar(eq[:, :], in_tile[:, :], float(2 * P), None, ALU.is_lt))
            own.link(v.tensor_scalar(tmp[:, 0:1], pidx[:, 0:1], float(KEYS), None, ALU.add))
            own.link(v.tensor_scalar(pos[:, :], key[:, :], tmp[:, 0:1], None, ALU.subtract))
            own.link(v.tensor_tensor(pos[:, :], pos[:, :], eq[:, :], ALU.mult))
            own.link(v.tensor_scalar(pos[:, :], pos[:, :], tmp[:, 0:1], None, ALU.add))
            v.tensor_copy(add_i[:, :], pos[:, :]).then_inc(cidx_ready, 1)

            def row_stats(c, i, s):
                dve.wait_ge(xc_in[s], arrived(c, i, s))
                for j in range(CW):
                    own.mark(v.bn_stats(st6[:, j, :], xc[:, s, j, :]))
                dve.wait_ge(dve_own, own.count)
                dve.sem_inc(dve_idle, 1)
                for j in range(CW):
                    own.mark(v.bn_aggr(mv[:, j, :], st6[:, j, :]))
                dve.wait_ge(dve_own, own.count)
                wait(dve, sd_ready, c)
                v.tensor_scalar(ve[:, :], mv[:, :, 1], LN_EPS, None, ALU.add).then_inc(ve_ready, 1)
                wait(dve, h_ready, c - 1)
                dve.wait_ge(sd_ready, c + 1)
                own.link(v.reciprocal(rstd[:, s, :], sd[:, :]))
                v.scalar_tensor_tensor(nmr[:, s, :], mv[:, :, 0], -1.0, rstd[:, s, :], ALU.mult, ALU.mult).then_inc(rs_ready, 1)

            def out_rows(c, s, l, n_stored):
                wait(dve, o_out[s], n_stored)
                k = c * NGR + l * NC * NGR
                for g, (a, w) in enumerate(groups_of(CW)):
                    dve.wait_ge(o_ps, k + (g + 1))
                    v.tensor_tensor(oc[:, s, a:a + w, :], ps_o[(s + g) % 2][:, 0:w * D].rearrange("p (w d) -> p w d", d=D),
                                    bias_b[:, l, :].unsqueeze(1).to_broadcast([P, w, D]), ALU.add).then_inc(o_ready, 1)

            def node_pass_0(c, i, s):
                row_stats(c, i, s)
                if isinstance(c, int) and c == 0:
                    return
                if s:
                    out_rows(c - 1, 0, 0, i * 16)
                else:
                    out_rows(c - 1, 1, 0, i * 16 - 16)
            chunks(dve, node_pass_0, own)
            out_rows(NC - 1, (NC - 1) % 2, 0, 16 * ((NC - 1) // 2))

            dve.wait_ge(total_ready, 1)
            own.link(v.tensor_scalar(total[:, :], total[:, :], 1.0, None, ALU.max))
            v.reciprocal(inv[:, :], total[:, :]).then_inc(inv_ready, 1)

            for l in range(L):
                def half(g, i, s, q, gl, l=l):
                    hh = 2 * g + q
                    bank = ps_t[q]
                    cols = slice(q * H, (q + 1) * H)
                    dve.wait_ge(d_ready, hh + 1)
                    wait(dve, ms_ready, hh - 1)
                    for j in range(H):
                        ins = v.tensor_scalar(sm[:, q, j * D:(j + 1) * D], bank[:, j * D:(j + 1) * D],
                                              xb[:, s, q * H + j, D + 1:D + 2], None, ALU.is_equal)
                        if l == 0:
                            own.mark(ins)
                        if j == H - 1:
                            if l == 0:
                                own.eng.wait_ge(own.sem, own.count)
                                dve.sem_inc(s_ready, 1)
                            else:
                                ins.then_inc(s_ready, 1)
                    if l == 0:
                        for j in range(H):
                            own.link(v.tensor_tensor_reduce(out=junk[:, :], in0=sm[:, q, j * D:(j + 1) * D], in1=rank_w[:, :],
                                                            scale=1.0, scalar=0.0, op0=ALU.mult, op1=ALU.add,
                                                            accum_out=rank_st[:, s, q * H + j:q * H + j + 1]))
                        own.link(v.tensor_scalar(first[:, :], rank_st[:, s, cols], float(2 * P), None, ALU.is_lt))
                        own.link(v.tensor_scalar(dsub[:, :], xb[:, s, cols, D + 1], repeat_row, None, ALU.subtract))
                        own.link(v.tensor_tensor(dsub[:, :], dsub[:, :], first[:, :], ALU.mult))
                        own.link(v.tensor_scalar(scat_idx[:, bass.ds(gl * G + q * H, H)], dsub[:, :], repeat_row, None, ALU.add))
                    dve.wait_ge(got[s][q], i * (16 * H) + 16 * H)
                    wait(dve, m_ready, hh - 1)
                    h4 = hb[:, s, cols, :]
                    t4 = tb[:, q, :].rearrange("p (w d) -> p w d", d=D)
                    if l == 1:
                        own.link(v.tensor_tensor(h4, h4, bn_b[:, 0, 0, :].unsqueeze(1).to_broadcast([P, H, D]), ALU.mult))
                        own.link(v.tensor_tensor(h4, h4, bn_b[:, 0, 1, :].unsqueeze(1).to_broadcast([P, H, D]), ALU.add))
                        v.scalar_tensor_tensor(t4, h4, 0.0, xb[:, s, cols, 0:D], ALU.max, ALU.add).then_inc(t_ready, 1)
                    else:
                        v.tensor_tensor(t4, h4, xb[:, s, cols, 0:D], ALU.add).then_inc(t_ready, 1)

                def group(g, i, s, gl, l=l):
                    half(g, i, s, 0, gl)
                    drain(g, s, 0, gl)
                    half(g, i, s, 1, gl)
                    drain(g, s, 1, gl)

                def drain(g, s, q, gl, l=l):
                    hh = 2 * g + q
                    if q == 0:
                        wait(dve, group_added, g - 1)
                    dve.sem_inc(dve_idle, 1)
                    own.link(v.tensor_copy(idx_st[:, s, q * H:(q + 1) * H], scat_idx[:, bass.ds(gl * G + q * H, H)]))
                    dve.wait_ge(y_ps, hh + 1)
                    v.tensor_copy(yb[:, s, q * H:(q + 1) * H, :].rearrange("p w d -> p (w d)"), ps_y[q][:, :]).then_inc(y_ready, 1)

                if l == 0:
                    repeat_col = sb("repeat_col", [P, 1])
                    repeat_row = repeat_col[:, 0:1]
                    own.link(v.tensor_scalar(repeat_row, pidx[:, :], float(REPEAT), None, ALU.add))
                if l == 1:
                    def node_pass_1(c, i, s):
                        if isinstance(c, int) and c < 2:
                            stored = 16 * plain_uses(s)
                        else:
                            stored = i * 16 + 16 * plain_uses(s)
                        out_rows(c, s, 1, stored)
                    even_chunks(dve, node_pass_1, own)

                def pair(i, l=l):
                    for s in range(2):
                        group(2 * i + (s + l * NG), i + l * NG // 2, s, 2 * i + s)
                pair_loop(dve, NG // 2, pair, own)

                def table_sum(c, i, s, l=l):
                    dve.wait_ge(ab_in[s], i * 32 + (32 + 32 * plain_uses(s) * l))
                    if l == 0:
                        if isinstance(c, int) and c < 2:
                            dve.wait_ge(o_out[s], 16 * plain_uses(s))
                        wait(dve, sum_out[s], i * 16)
                    else:
                        if isinstance(c, int) and c < 2:
                            dve.wait_ge(o_out[s], 32 * plain_uses(s))
                        wait(dve, sum_out[s], i * 16 + 16 * plain_uses(s))
                    if not (isinstance(c, int) and c < 2 and l == 0):
                        dve.wait_ge(st_ps, (c - 1) * NGR + l * NC * NGR)
                    flat = "p c d -> p (c d)"
                    v.tensor_tensor(oc[:, s, :, :].rearrange(flat), xc[:, s, :, :].rearrange(flat),
                                    yc[:, s, :, :].rearrange(flat), ALU.add).then_inc(sum_ready, 1)
                    for g, (a, w) in enumerate(stat_groups(c)):
                        k = c * NGR + (l * NC * NGR + g + 1)
                        dve.wait_ge(st_ps, k)
                        n = P if a + w <= valid(c) else P - 1
                        v.bn_stats(bst[:, g % 2, :], ps_t[(s + g) % 2][:, 0:w * D].rearrange("p (w d) -> p w d", d=D)[:, :, 0:n]) \
                            .then_inc(st_read, 1)
                        dve.wait_ge(st_read, k)
                        own.mark(v.tensor_copy(bstat[:, bass.ds(c * NGR + g, 1), :].rearrange("p u k -> p (u k)"), bst[:, g % 2, :]))
                chunks(dve, table_sum, own)
                dve.wait_ge(dve_own, own.count)
                own.link(v.bn_aggr(bmv[:, :], bstat[:, 0:NC * NGR, :].rearrange("p n k -> p (n k)")))
                v.tensor_scalar(bsd[:, :], bmv[:, 1:2], BN_EPS, None, ALU.add).then_inc(bn_var, 1)
                dve.wait_ge(bn_sd, l + 1)
                own.link(v.reciprocal(brs[:, :], sd[:, 0:1]))
                own.link(v.tensor_tensor(bn_col[:, l, 0:1], brs[:, :], vec[:, 3 * l + 1:3 * l + 2], ALU.mult))
                own.link(v.tensor_tensor(tmp[:, 0:1], bmv[:, 0:1], bn_col[:, l, 0:1], ALU.mult))
                v.tensor_tensor(bn_col[:, l, 1:2], vec[:, 3 * l + 2:3 * l + 3], tmp[:, 0:1], ALU.subtract).then_inc(bn_ready, 1)
                dve.wait_ge(bnb_ps, l + 1)
                v.tensor_copy(bn_b[:, l, :, :].rearrange("p k d -> p (k d)"), ps_t[0][:, 0:2 * D]).then_inc(bnb_ready, 1)

            dve.wait_ge(bnb_ready, L)

            def final(c, i, s):
                if isinstance(c, int) and c < 2:
                    dve.wait_ge(sum_out[s], 32 * plain_uses(s))
                if not isinstance(c, int):
                    dve.wait_ge(f_in[s], i * 32 + 32)
                    dve.wait_ge(f_out[s], i * 16)
                else:
                    dve.wait_ge(f_in[s], arrived(c, i, s) + 16 * (c // 2 + 1))
                    wait(dve, f_out[s], arrived(c - 2, i, s) if c >= 2 else 0)
                x3, o3 = xc[:, s, :, :], oc[:, s, :, :]
                own.link(v.tensor_tensor(x3, x3, bn_b[:, 1, 0, :].unsqueeze(1).to_broadcast([P, CW, D]), ALU.mult))
                own.link(v.tensor_tensor(x3, x3, bn_b[:, 1, 1, :].unsqueeze(1).to_broadcast([P, CW, D]), ALU.add))
                v.tensor_tensor(o3, x3, yc[:, s, :, :], ALU.add).then_inc(f_ready, 1)
            chunks(dve, final, own)

        @block.scalar
        def _(act):
            a_ = nc.scalar
            act.wait_ge(blank, 3)
            for c in range(min(2, NC)):
                row_dma(act, xc[:, c % 2, :, :], x, c, xc_in[c % 2], True)

            def node_pass_0(c, i, s):
                act.wait_ge(ve_ready, c + 1)
                a_.activation(sd[:, :], ve[:, :], ACT.Sqrt).then_inc(sd_ready, 1)
                act.wait_ge(rs_ready, c + 1)
                wait(act, h_out[s], i * 16)
                if not isinstance(c, int) or c >= 2:
                    act.wait_ge(tr_ready, c * NGR - NGR)
                for j in range(CW):
                    ins = a_.activation(yc[:, s, j, :], xc[:, s, j, :], ACT.Relu, scale=rstd[:, s, j:j + 1], bias=nmr[:, s, j:j + 1])
                ins.then_inc(h_ready, 1)
                act.wait_ge(h_ready, c + 1)
                table_dma(act, yc[:, s, :, :], h_tab[0], c, h_out[s], False)
                if not isinstance(c, int) or c + 2 < NC:
                    row_dma(act, xc[:, s, :, :], x, c + 2, xc_in[s], True)
                if isinstance(c, int) and c == 0:
                    return
                turned(c - 1, 1 - s)
                if isinstance(c, int) and c == 1:
                    return
                act.wait_ge(o_ready, c * NGR - NGR)
                table_dma(act, oc[:, s, :, :], acc[0][0], c - 2, o_out[s], False)

            def turned(c, s):
                for g, (a, w) in enumerate(groups_of(CW)):
                    act.wait_ge(tr_ready, c * NGR + (g + 1))
                    a_.activation(ht[:, (s + g) % 2, 0:w * D], ps_t[(s + g) % 2][:, 0:w * D], ACT.Copy).then_inc(ht_ready, 1)

            def full_pairs(eng, body):
                pairs = max(0, (FULL - 2) // 2)

                def pair(i):
                    for s in range(2):
                        body(2 * i + s, i, s)
                pair_loop(eng, pairs, pair)
                for c in range(2 * pairs, NC):
                    body(c, c // 2, c % 2)
            full_pairs(act, node_pass_0)
            turned(NC - 1, (NC - 1) % 2)
            for c in (NC - 2, NC - 1):
                act.wait_ge(o_ready, (c + 1) * NGR)
                table_dma(act, oc[:, c % 2, :, :], acc[0][0], c, o_out[c % 2], False)

            for l in range(L):
                if l == 1:
                    act.wait_ge(bnb_ready, 1)
                    for s in range(2):
                        act.wait_ge(sum_out[s], 16 * plain_uses(s))

                    def load(c, s):
                        table_dma(act, xc[:, s, :, :], h_tab[1], c, xc_in[s], True)
                    for c in range(2):
                        load(c, c)

                    def node_pass_1(c, i, s):
                        for g, (a, w) in enumerate(groups_of(CW)):
                            act.wait_ge(tr_ready, c * NGR + (NC * NGR + g + 1))
                            if g == NGR - 1 and (not isinstance(c, int) or c + 2 < NC):
                                load(c + 2, s)
                            a_.activation(ht[:, (s + g) % 2, 0:w * D], ps_t[(s + g) % 2][:, 0:w * D], ACT.Relu,
                                          scale=bn_col[:, 0, 0:1], bias=bn_col[:, 0, 1:2]).then_inc(ht_ready, 1)
                        if isinstance(c, int) and c == 0:
                            return
                        act.wait_ge(o_ready, c * NGR + NC * NGR)
                        table_dma(act, oc[:, 1 - s, :, :], acc[1][0], c - 1, o_out[1 - s], False)
                    pairs = (NC - 2) // 2

                    def pair(i):
                        for s in range(2):
                            node_pass_1(2 * i + s, i, s)
                    pair_loop(act, pairs, pair)
                    for c in range(2 * pairs, NC):
                        node_pass_1(c, c // 2, c % 2)
                    act.wait_ge(o_ready, 2 * NC * NGR)
                    table_dma(act, oc[:, (NC - 1) % 2, :, :], acc[1][0], NC - 1, o_out[(NC - 1) % 2], False)

                def half(g, s, q):
                    hh = 2 * g + q
                    act.wait_ge(t_ready, hh + 1)
                    wait(act, ms_ready, hh - 1)
                    for j in range(H):
                        ins = a_.activation(mb[:, q, j * D:(j + 1) * D], tb[:, q, j * D:(j + 1) * D], ACT.Relu,
                                            scale=xb[:, s, q * H + j, D + 2:D + 3])
                    ins.then_inc(m_ready, 1)
                    act.wait_ge(ms_ready, hh + 1)
                    wait(act, y_ps, hh - 1)
                    a_.activation(mt[:, q, :], ps_m[q][:, :], ACT.Copy).then_inc(mt_ready, 1)

                def pair_e(i, l=l):
                    for s in range(2):
                        for q in range(2):
                            half(2 * i + (s + l * NG), s, q)
                pair_loop(act, NG // 2, pair_e)

                to = h_tab[1] if l == 0 else sum_rows

                def store(c, i, s, l=l, to=to):
                    act.wait_ge(sum_ready, c + (1 + l * NC))
                    table_dma(act, oc[:, s, :, :], to, c, sum_out[s], False)
                even_chunks(act, store)
                act.wait_ge(bn_var, l + 1)
                a_.activation(sd[:, 0:1], bsd[:, :], ACT.Sqrt).then_inc(bn_sd, 1)

            def final(c, i, s):
                act.wait_ge(f_ready, c + 1)
                row_dma(act, oc[:, s, :, :], out, c, f_out[s], False)
            chunks(act, final)

        @block.tensor
        def _(pe):
            te = nc.tensor

            def on_all(dst, col):
                return te.matmul(dst, col.to_broadcast([P, P]), ident[:, :], start=True, stop=True)

            pe.wait_ge(consts, 5)
            pe.wait_ge(params_in, 16 * 5 * L)
            pe.wait_ge(tot_ready, 1)
            te.matmul(ps_t[0][:, 0:R], before_p[:, :], tot[:, :], start=True, stop=True)
            te.matmul(ps_t[0][:, R:2 * R], ones[:, :], tot[:, :], start=True, stop=True)
            for l in range(L):
                last = on_all(ps_t[0][:, (l + 1) * D:(l + 2) * D], vec[:, 3 * l:3 * l + 1])
            last.then_inc(off_ready, 1)
            pe.wait_ge(off_read, 1)

            def keys(c, i, s):
                pe.wait_ge(kst_ready, c + 1)
                for g, (a, w) in enumerate(groups_of(CW)):
                    k = c * NGR + g
                    if isinstance(c, int) and c == 0:
                        wait(pe, keyb_read, g - 1)
                    else:
                        pe.wait_ge(keyb_read, k if g == 0 else k - 1)
                    for j in range(w):
                        last = on_all(ps_t[g % 2][:, j * D:(j + 1) * D], key_st[:, s, a + j:a + j + 1])
                    last.then_inc(keyb_ready, 1)
            even_chunks(pe, keys)
            pe.wait_ge(keyb_read, NC * NGR)
            pe.wait_ge(types_ready, 1)

            def node_products(l, ready):
                def chunk(c, i, s):
                    ready(c, i, s)
                    source = (yc if l == 0 else xc)[:, s, :, :]
                    gs = groups_of(CW)

                    def turn(g):
                        a, w = gs[g]
                        for j in range(w):
                            last = te.transpose(ps_t[(s + g) % 2][:, j * D:(j + 1) * D], source[:, a + j, :], ident[:, :])
                        last.then_inc(tr_ready, 1)

                    def product(g):
                        a, w = gs[g]
                        k = c * NGR + (l * NC * NGR + g)
                        pe.wait_ge(ht_ready, k + 1)
                        wait(pe, o_ready, k - 1)
                        for j in range(w):
                            last = te.matmul(ps_o[(s + g) % 2][:, j * D:(j + 1) * D], ht[:, (s + g) % 2, j * D:(j + 1) * D],
                                             root_sb[:, l * D:(l + 1) * D], start=True, stop=True)
                        last.then_inc(o_ps, 1)
                    turn(0)
                    for g in range(1, NGR):
                        turn(g)
                        product(g - 1)
                    product(NGR - 1)
                return chunk

            chunks(pe, node_products(0, lambda c, i, s: pe.wait_ge(h_ready, c + 1)))

            for l in range(L):
                if l == 1:
                    def rows_in(c, i, s):
                        pe.wait_ge(xc_in[s], i * 16 + (16 + arrived(NC - 1 - (NC - 1 - s) % 2, 0, s)))
                    even_chunks(pe, node_products(1, rows_in))
                    pe.wait_ge(ht_ready, 2 * NC * NGR)

                def half(g, i, s, q, gl, l=l):
                    hh = 2 * g + q
                    if q == 0:
                        pe.wait_ge(xb_in[s], i * 16 + 16)
                    wait(pe, s_ready, hh - 1)
                    for j in range(H):
                        last = on_all(ps_t[q][:, j * D:(j + 1) * D], xb[:, s, q * H + j, D + 1:D + 2])
                    last.then_inc(d_ready, 1)
                    pe.wait_ge(s_ready, hh + 1)
                    pe.wait_ge(m_ready, hh + 1)
                    wait(pe, mt_ready, hh - 1)
                    for j in range(H):
                        c = slice(j * D, (j + 1) * D)
                        last = te.matmul(ps_m[q][:, c], mb[:, q, c], sm[:, q, c], start=True, stop=True)
                    last.then_inc(ms_ready, 1)
                    pe.wait_ge(mt_ready, hh + 1)
                    wait(pe, y_ready, hh - 1)
                    for j in range(H):
                        c = slice(j * D, (j + 1) * D)
                        kind = pe.value_load(tile_type_i[0:1, bass.ds(gl * G + (q * H + j), 1)], min_val=0, max_val=R - 1)
                        last = te.matmul(ps_y[q][:, c], mt[:, q, c], w_sb[l][:, bass.ds(kind * D, D)], start=True, stop=True)
                    last.then_inc(y_ps, 1)

                def pair(i, l=l):
                    for s in range(2):
                        for q in range(2):
                            half(2 * i + (s + l * NG), i + l * NG // 2, s, q, 2 * i + s)
                pair_loop(pe, NG // 2, pair)

                def feature_rows(c, i, s, l=l):
                    pe.wait_ge(sum_ready, c + (1 + l * NC))
                    for g, (a, w) in enumerate(stat_groups(c)):
                        if isinstance(c, int) and 2 * c + g < 2 and c == 0:
                            pass
                        else:
                            wait(pe, st_read, c * NGR + (g - 1 + l * NC * NGR))
                        for j in range(w):
                            last = te.transpose(ps_t[(s + g) % 2][:, j * D:(j + 1) * D], oc[:, s, a + j, :], ident[:, :])
                        last.then_inc(st_ps, 1)
                chunks(pe, feature_rows)
                pe.wait_ge(bn_ready, l + 1)
                for k in range(2):
                    last = on_all(ps_t[0][:, k * D:(k + 1) * D], bn_col[:, l, k:k + 1])
                last.then_inc(bnb_ps, 1)
                pe.wait_ge(bnb_ready, l + 1)


_INS = ['x', 'src', 'dst', 'edge_attr_128', 'edge_type_8', 'L0_gnn_weight', 'L0_gnn_root', 'L0_gnn_bias',
        'L0_gnn_bn_gamma', 'L0_gnn_bn_beta']


def kernel(**inputs):
    import numpy as _np
    import concourse.bacc as _bacc
    from concourse import mybir as _mybir
    from concourse.bass_utils import run_bass_kernel_spmd as _run

    nc = _bacc.Bacc("TRN2", target_bir_lowering=False, num_devices=1)
    arrays, args = {}, []
    for name in _INS:
        a = _np.ascontiguousarray(inputs[name])
        arrays[f"in_{name}_dram"] = a
        args.append(nc.dram_tensor(f"in_{name}_dram", a.shape, _mybir.dt.from_np(a.dtype), kind="ExternalInput").ap())
    out = nc.dram_tensor("out_0_dram", inputs["x"].shape, _mybir.dt.float32, kind="ExternalOutput").ap()
    gnn_kernel(nc, *args, out)
    r = _run(nc, [arrays], core_ids=[0])
    return r.results[0]["out_0_dram"]
```

```python
import concourse.bass as bass
from concourse import mybir
from contextlib import ExitStack

P = 128
FP32 = mybir.dt.float32
I32 = mybir.dt.int32
U32 = mybir.dt.uint32
ALU = mybir.AluOpType
ACT = mybir.ActivationFunctionType
BN_EPS = 1e-5
LN_EPS = 1e-5


def divisor_up_to(n, most):
    return max(k for k in range(1, most + 1) if n % k == 0)


def wait(eng, sem, value):
    if isinstance(value, int) and value <= 0:
        return
    eng.wait_ge(sem, value)


class Chain:

    def __init__(self, eng, sem):
        self.eng, self.sem, self.count = eng, sem, 0

    def mark(self, instruction):
        instruction.then_inc(self.sem, 1)
        self.count = self.count + 1

    def link(self, instruction):
        self.mark(instruction)
        self.eng.wait_ge(self.sem, self.count)


def pair_loop(eng, pairs, body, chain=None):
    if not pairs:
        return
    before = chain.count if chain else 0
    body(0)
    step = chain.count - before if chain else 0
    if pairs > 1:
        with eng.Fori(1, pairs) as i:
            if chain:
                chain.count = i * step + before
            body(i)
        if chain:
            chain.count = before + step * pairs


def ends_loop(eng, turns, body, chain=None):
    pair_loop(eng, turns - 1, lambda i: body(i, False), chain)
    body(turns - 1, True)


def gnn_kernel(nc, x, src, dst, edge_attr, edge_type, weight, root, bias, gamma, beta, out):
    N, D = x.shape
    E = src.shape[0]
    L, R = weight.shape[0], weight.shape[1]
    assert D == P and edge_attr.shape == (E, D) and L == 2

    F = -(-N // P)
    FE = -(-E // P)
    assert F == FE
    CW = divisor_up_to(F, 17)
    NC = F // CW
    PV = N - (P - 1) * F
    assert E == N and 0 < PV <= F
    FULL = PV // CW
    ROWS = P * (F + 2)
    REPEAT = P * F
    PADDST = P * (F + 1)
    G = 8
    H = 4
    NT = -(-((E + R * (P - 1)) // P) // (2 * G)) * 2 * G
    NG = NT // G
    TAIL = NT - E // P
    M = D + 4
    KEYS = (R + 1) * ROWS
    BIG = float(1 << 22)

    def valid(c):
        return max(0, min(CW, PV - c * CW)) if isinstance(c, int) else CW

    def n_dma(c):
        v = valid(c)
        return 1 if v == CW else 3 if v else 2

    def arrived(c, i, s):
        if not isinstance(c, int):
            return i * 16 + 16
        return 16 * sum(n_dma(k) for k in range(s, c + 1, 2))

    def groups_of(cols):
        return [(a, min(H, cols - a)) for a in range(0, cols, H)]

    NGR = len(groups_of(CW))

    ctx = ExitStack()
    with ctx:
        def sb(name, shape, dt=FP32):
            return ctx.enter_context(nc.sbuf_tensor(name, shape, dt))

        def pb(name):
            return ctx.enter_context(nc.psum_tensor(name, [P, H * D], FP32))

        def sem(name):
            return ctx.enter_context(nc.semaphore(name))

        def dram(name, shape):
            return nc.dram_tensor(name, shape, FP32, kind="Internal").ap()

        h_tab = [dram("h0_rows", [P * F, D]), dram("h1_rows", [P * F, D])]
        acc = [[dram(f"acc_{l}_{k}", [ROWS, D]) for k in range(2)] for l in range(L)]
        sorted_rows = dram("sorted_rows", [NT * P, M])
        key_count = dram("key_count", [KEYS + P, 1])
        sum_rows = dram("sum_rows", [P * F, D])

        ident = sb("ident", [P, P])
        ones = sb("ones", [P, P])
        before_p = sb("before_p", [P, P])
        rank_w = sb("rank_w", [P, P])
        pidx = sb("pidx", [P, 1])
        pidx_i = sb("pidx_i", [P, 1], I32)
        zeros = sb("zeros", [P, CW * D])
        tiota_i = sb("tiota_i", [1, NT], I32)
        tiota = sb("tiota", [1, NT])
        w_sb = [sb(f"w_sb{l}", [P, R * D]) for l in range(L)]
        root_sb = sb("root_sb", [P, L * D])
        vec = sb("vec", [P, 6])
        bias_b = sb("bias_b", [P, L, D])
        bn_col = sb("bn_col", [P, L, 2])
        bn_b = sb("bn_b", [P, L, 2, D])

        type_i = sb("type_i", [P, FE], I32)
        src_i = sb("src_i", [P, FE], I32)
        dst_i = sb("dst_i", [P, FE], I32)
        type_f = sb("type_f", [P, FE])
        dst_x = sb("dst_x", [P, FE + 2])
        dst_f = dst_x[:, 1:FE + 1]
        near_i = sb("near_i", [P, 2], I32)
        as_prev = sb("as_prev", [P, FE])
        as_next = sb("as_next", [P, FE])
        tails = sb("tails", [P, 2, R])
        through = sb("through", [P, 2])
        carry_in = sb("carry_in", [P, 2, R])
        row_in = sb("row_in", [R, 4, P])
        row_carry = sb("row_carry", [R, 2, P + 1])
        falls = sb("falls", [P, 1])
        flag_i = sb("flag_i", [1, 1], I32)
        run = sb("run", [P, FE])
        key = sb("key", [P, FE])
        key_i = sb("key_i", [P, FE], U32)
        add_i = sb("add_i", [P, FE], U32)
        in_tile = sb("in_tile", [P, FE])
        total = sb("total", [P, FE])
        inv = sb("inv", [P, FE])
        pos = sb("pos", [P, FE])
        pos_i = sb("pos_i", [P, FE], U32)
        cum = sb("cum", [P, R, FE])
        eq = sb("eq", [P, FE])
        tmp = sb("tmp", [P, FE])
        zcol = sb("zcol", [P, FE])
        tot = sb("tot", [P, R])
        off = sb("off", [P, R])
        grand = sb("grand", [P, R])
        ntile = sb("ntile", [P, R])
        ntile_i = sb("ntile_i", [P, R], I32)
        ends = sb("ends", [P, R])
        base = sb("base", [P, R])
        padn = sb("padn", [P, R])
        padpos = sb("padpos", [P, R + TAIL])
        padpos_i = sb("padpos_i", [P, R + TAIL], U32)
        padrow = sb("padrow", [P, M])
        tile_type = sb("tile_type", [1, NT])
        tile_type_i = sb("tile_type_i", [1, NT], I32)
        scat_idx = sb("scat_idx", [P, NT], U32)

        key_st = sb("key_st", [P, 2, CW])
        same = sb("same", [P, 2, D])
        junk = sb("junk", [P, D])
        val_st = sb("val_st", [P, 2, CW])
        cnt_idx = sb("cnt_idx", [P, 2, CW], U32)
        cnt_val = sb("cnt_val", [P, 2, CW])
        meta = sb("meta", [P, 2, CW, M])
        pos_st = sb("pos_st", [P, 2, CW], U32)
        xc = sb("xc", [P, 2, CW, D])
        yc = sb("yc", [P, 2, CW, D])
        oc = sb("oc", [P, 2, CW, D])
        st6 = sb("st6", [P, CW, 6])
        mv = sb("mv", [P, CW, 2])
        ve = sb("ve", [P, CW])
        sd = sb("sd", [P, CW])
        rstd = sb("rstd", [P, 2, CW])
        nmr = sb("nmr", [P, 2, CW])
        ht = sb("ht", [P, 2, H * D])
        xb = sb("xb", [P, 2, G, M])
        src_st = sb("src_st", [P, 2, G], U32)
        hb = sb("hb", [P, 2, G, D])
        sm = sb("sm", [P, 2, H * D])
        tb = sb("tb", [P, 2, H * D])
        mb = sb("mb", [P, 2, H * D])
        mt = sb("mt", [P, 2, H * D])
        yb = sb("yb", [P, 2, G, D])
        rank_st = sb("rank_st", [P, 2, G])
        first = sb("first", [P, H])
        dsub = sb("dsub", [P, H])
        idx_f = sb("idx_f", [P, H])
        idx_st = sb("idx_st", [P, 2, G], U32)
        NST = NC * NGR + NGR
        bstat = sb("bstat", [P, NST, 6])
        bst = sb("bst", [P, 2, 6])
        bmv = sb("bmv", [P, 2])
        bsd = sb("bsd", [P, 1])
        brs = sb("brs", [P, 1])

        ps_t = [pb("ps_t0"), pb("ps_t1")]
        ps_o = [pb("ps_o0"), pb("ps_o1")]
        ps_m = [pb("ps_m0"), pb("ps_m1")]
        ps_y = [pb("ps_y0"), pb("ps_y1")]

        consts = sem("consts")
        pool_own = sem("pool_own")
        dve_own = sem("dve_own")
        act_own = sem("act_own")
        dve_idle = sem("dve_idle")
        idle = sem("idle")
        params_in = sem("params_in")
        idx_in = sem("idx_in")
        blank = sem("blank")
        tot_ready = sem("tot_ready")
        off_ready = sem("off_ready")
        off_read = sem("off_read")
        bias_ps = sem("bias_ps")
        types_ready = sem("types_ready")
        pos_ready = sem("pos_ready")
        tables_zero = sem("tables_zero")
        kst_ready = sem("kst_ready")
        keyb_ready = sem("keyb_ready")
        keyb_read = sem("keyb_read")
        cidx_ready = sem("cidx_ready")
        chain_sem = sem("chain_sem")
        cnt_got = sem("cnt_got")
        total_ready = sem("total_ready")
        tails_ready = sem("tails_ready")
        rows_ps = sem("rows_ps")
        carries_ready = sem("carries_ready")
        carries_ps = sem("carries_ps")
        flag_ready = sem("flag_ready")
        branch_own = sem("branch_own")
        pool_branch = sem("pool_branch")
        inv_ready = sem("inv_ready")
        attr_in = [sem("attr_in0"), sem("attr_in1")]
        sorted_out = [sem("sorted_out0"), sem("sorted_out1")]
        pads_out = sem("pads_out")
        xc_in = [sem("xc_in0"), sem("xc_in1")]
        ve_ready = sem("ve_ready")
        sd_ready = sem("sd_ready")
        rs_ready = sem("rs_ready")
        h_ready = sem("h_ready")
        h_out = [sem("h_out0"), sem("h_out1")]
        tr_ready = sem("tr_ready")
        ht_ready = sem("ht_ready")
        o_ps = sem("o_ps")
        o_ready = sem("o_ready")
        o_out = [sem("o_out0"), sem("o_out1")]
        xb_in = [[sem(f"xb_in{s}{q}") for q in range(2)] for s in range(2)]
        src_ready = sem("src_ready")
        got = [[sem(f"got{s}{q}") for q in range(2)] for s in range(2)]
        d_ready = sem("d_ready")
        s_ready = sem("s_ready")
        t_ready = sem("t_ready")
        m_ready = sem("m_ready")
        ms_ready = sem("ms_ready")
        mt_ready = sem("mt_ready")
        y_ps = sem("y_ps")
        y_ready = sem("y_ready")
        added = [sem("added0"), sem("added1")]
        half_added = sem("half_added")
        ab_in = [sem("ab_in0"), sem("ab_in1")]
        sum_ready = sem("sum_ready")
        sum_out = [sem("sum_out0"), sem("sum_out1")]
        st_ps = sem("st_ps")
        st_read = sem("st_read")
        bn_var = sem("bn_var")
        bn_sd = sem("bn_sd")
        bn_ready = sem("bn_ready")
        bnb_ps = sem("bnb_ps")
        bnb_ready = sem("bnb_ready")
        f_in = [sem("f_in0"), sem("f_in1")]
        f_ready = sem("f_ready")
        f_out = [sem("f_out0"), sem("f_out1")]

        block = ctx.enter_context(nc.Block())

        def by_partition(a, rows):
            return bass.AP(a.tensor, 0, [[F * D, P], [1, rows * D]])

        def row_dma(eng, tile, a, c, semaphore, load):
            v = valid(c)
            if v == CW:
                far = by_partition(a, PV)[:, bass.ds(c * (CW * D), CW * D)].rearrange("p (c d) -> p c d", d=D)
                pieces = [(tile, far)]
            else:
                far = bass.AP(a.tensor, c * CW * D, [[F * D, P - 1], [D, CW], [1, D]])
                pieces = [(tile[0:112], far[0:112]), (tile[112:P - 1], far[112:P - 1])]
                if v:
                    far = bass.AP(a.tensor, (P - 1) * F * D + c * CW * D, [[F * D, 1], [D, v], [1, D]])
                    pieces.append((tile[P - 1:P, 0:v], far))
            for near, far in pieces:
                o, i = (near, far) if load else (far, near)
                eng.dma_start(o, i).then_inc(semaphore, 16)

        def table_dma(eng, tile, a, c, semaphore, load):
            far = by_partition(a, F)[:, bass.ds(c * (CW * D), CW * D)]
            near = tile.rearrange("p c d -> p (c d)")
            o, i = (near, far) if load else (far, near)
            eng.dma_start(o, i).then_inc(semaphore, 16)

        def chunks(eng, body, chain=None):
            pairs = FULL // 2

            def pair(i):
                for s in range(2):
                    body(2 * i + s, i, s)
            pair_loop(eng, pairs, pair, chain)
            for c in range(2 * pairs, NC):
                body(c, c // 2, c % 2)

        def even_chunks(eng, body, chain=None):
            pairs = NC // 2

            def pair(i):
                for s in range(2):
                    body(2 * i + s, i, s)
            pair_loop(eng, pairs, pair, chain)
            for c in range(2 * pairs, NC):
                body(c, c // 2, c % 2)

        def last_count(slot):
            return arrived(NC - 1 - (NC - 1 - slot) % 2, 0, slot)

        def plain_uses(slot):
            return (NC - slot + 1) // 2

        def stat_groups(c):
            gs = groups_of(CW)
            v = valid(c)
            if v in (0, CW):
                return gs
            cut = [(a, w) for a, w in [(0, v)] if w <= H] + [(a + v, w) for a, w in groups_of(CW - v)]
            assert v <= H and len(cut) == NGR
            return cut

        @block.sync
        def _(sp):
            with nc.allow_non_contiguous_dma(reason="one column of parameters, once"):
                for l in range(L):
                    for k, a in enumerate((bias, gamma, beta)):
                        sp.dma_start(vec[:, 3 * l + k:3 * l + k + 1], a[l, :].rearrange("(d u) -> d u", u=1)).then_inc(params_in, 16)
            for l in range(L):
                sp.dma_start(w_sb[l][:, :].rearrange("d (r o) -> d r o", r=R), weight[l].rearrange("r d o -> d r o")).then_inc(params_in, 16)
                sp.dma_start(root_sb[:, l * D:(l + 1) * D], root[l]).then_inc(params_in, 16)
            sp.wait_ge(blank, 1)
            for near, far in ((type_i, edge_type), (src_i, src), (dst_i, dst)):
                for a, b in ((0, 112), (112, P - 1)):
                    sp.dma_start(near[a:b, :], bass.AP(far.tensor, a * FE, [[FE, b - a], [1, FE]])).then_inc(idx_in, 16)
                sp.dma_start(near[P - 1:P, 0:PV], bass.AP(far.tensor, (P - 1) * FE, [[FE, 1], [1, PV]])).then_inc(idx_in, 16)
            with nc.allow_non_contiguous_dma(reason="one column of indices, once"):
                sp.dma_start(near_i[1:P, 0:1], bass.AP(dst.tensor, FE - 1, [[FE, P - 1], [1, 1]])).then_inc(idx_in, 16)
                sp.dma_start(near_i[0:P - 1, 1:2], bass.AP(dst.tensor, FE, [[FE, P - 1], [1, 1]])).then_inc(idx_in, 16)
            sp.wait_ge(blank, 2)
            n = (KEYS + P) // P
            flat = key_count.rearrange("(p c) u -> p (c u)", p=P)
            for a in range(0, n, CW * D):
                b = min(n, a + CW * D)
                sp.dma_start(flat[:, a:b], zeros[:, 0:b - a]).then_inc(tables_zero, 16)
            for l in range(L):
                sp.dma_start(acc[l][0][P * F:ROWS, :].rearrange("(p c) d -> p (c d)", p=P), zeros[:, 0:2 * D]).then_inc(tables_zero, 16)
                sp.dma_start(acc[l][1][P * F:ROWS, :].rearrange("(p c) d -> p (c d)", p=P), zeros[:, 0:2 * D]).then_inc(tables_zero, 16)
                for c in range(NC):
                    table_dma(sp, zeros[:, :].rearrange("p (c d) -> p c d", d=D), acc[l][1], c, tables_zero, False)

            def attrs(c, i, s):
                wait(sp, sorted_out[s], i * (16 * CW))
                row_dma(sp, meta[:, s, :, 0:D], edge_attr, c, attr_in[s], True)
            sp.wait_ge(blank, 3)
            chunks(sp, attrs)

            for l in range(L):
                if l == 0:
                    for s in range(2):
                        sp.wait_ge(sorted_out[s], 16 * CW * plain_uses(s))
                    sp.wait_ge(pads_out, 16 * (R + TAIL))

                def rows(i, l=l):
                    for s in range(2):
                        for q in range(2):
                            hh = 4 * i + (2 * s + q + l * 2 * NG)
                            wait(sp, m_ready, hh - 3)
                            far = sorted_rows[bass.ds((4 * i + (2 * s + q)) * (H * P), H * P), :].rearrange("(g p) c -> p g c", p=P)
                            sp.dma_start(xb[:, s, q * H:(q + 1) * H, :], far).then_inc(xb_in[s][q], 16)
                pair_loop(sp, NG // 2, rows)

                for k in range(2):
                    sp.wait_ge(added[k], 16 * (l + 1) * NT // 2)
                if l == 1:
                    sp.wait_ge(o_ready, 2 * NC * NGR)
                    sp.wait_ge(tr_ready, 2 * NC * NGR)

                def ab(c, i, s, l=l):
                    if not isinstance(c, int) or c >= 2:
                        sp.wait_ge(sum_ready, c + (l * NC - 1))
                    table_dma(sp, xc[:, s, :, :], acc[l][0], c, ab_in[s], True)
                    table_dma(sp, yc[:, s, :, :], acc[l][1], c, ab_in[s], True)

                if l == 0:
                    for s in range(2):
                        sp.wait_ge(h_out[s], 16 * plain_uses(s))
                    sp.wait_ge(o_ps, NC * NGR)
                even_chunks(sp, ab)
                if l == 1:
                    break
            for s in range(2):
                sp.wait_ge(sum_out[s], 16 * 2 * plain_uses(s))
            sp.wait_ge(st_ps, 2 * NC * NGR)
            sp.wait_ge(bnb_ready, 2)

            def final(c, i, s):
                wait(sp, f_ready, c - 1)
                table_dma(sp, xc[:, s, :, :], sum_rows, c, f_in[s], True)
                row_dma(sp, yc[:, s, :, :], x, c, f_in[s], True)
            chunks(sp, final)
            for s in range(2):
                sp.wait_ge(f_out[s], last_count(s))

        @block.gpsimd
        def _(pool):
            own = Chain(pool, pool_own)
            gp = nc.gpsimd
            own.link(gp.memset(ident[:, :], 0.0))
            gp.affine_select(out=ident[:, :], in_=ident[:, :], compare_op=ALU.not_equal, fill=1.0, base=0,
                             pattern=[[-1, P]], channel_multiplier=1).then_inc(consts, 1)
            own.link(gp.memset(before_p[:, :], 1.0))
            gp.affine_select(out=before_p[:, :], in_=before_p[:, :], compare_op=ALU.is_gt, fill=0.0, base=0,
                             pattern=[[1, P]], channel_multiplier=-1).then_inc(consts, 1)
            own.link(gp.memset(rank_w[:, :], float(2 * P + 1)))
            gp.affine_select(out=rank_w[:, :], in_=rank_w[:, :], compare_op=ALU.is_gt, fill=1.0, base=0,
                             pattern=[[-1, P]], channel_multiplier=1).then_inc(consts, 1)
            gp.iota(pidx_i[:, :], pattern=[[0, 1]], base=0, channel_multiplier=1).then_inc(consts, 1)
            gp.iota(tiota_i[:, :], pattern=[[1, NT]], base=0, channel_multiplier=0).then_inc(consts, 1)

            def indexed(reg_waits, **kw):
                for s, v in reg_waits:
                    if isinstance(v, int):
                        wait(pool, s, v)
                    else:
                        pool.wait_ge(s, v)
                        pool.sem_inc(idle, 1)
                return pool.indirect_dma_start(**kw)

            def at(ap):
                return bass.IndirectOffsetOnAxis(ap=ap, axis=0)

            slow = Chain(pool, pool_branch)
            pool.wait_ge(flag_ready, 1)
            unsorted = pool.value_load(flag_i[0:1, 0:1], min_val=0, max_val=1)
            with pool.If(unsorted > 0):
                pool.wait_ge(cidx_ready, 1)
                n_key = -(-((KEYS + P) // P) // (CW * D))
                pool.wait_ge(tables_zero, 16 * (n_key + L * (2 + NC)))

                def count_chunk(c, i, s):
                    slow.mark(gp.tensor_copy(cnt_idx[:, s, :], add_i[:, bass.ds(c * CW, CW)]))
                    slow.link(gp.tensor_copy(cnt_val[:, s, :], in_tile[:, bass.ds(c * CW, CW)]))
                    pool.sem_inc(idle, 1)
                    for j in range(CW):
                        indexed([(chain_sem, c * (16 * CW) + 16 * j)], out=key_count, out_offset=at(cnt_idx[:, s, j:j + 1]),
                                in_=cnt_val[:, s, j:j + 1], in_offset=None, compute_op=ALU.add).then_inc(chain_sem, 16)
                even_chunks(pool, count_chunk, slow)
                pool.wait_ge(chain_sem, 16 * FE)

                def total_chunk(c, i, s):
                    slow.link(gp.tensor_copy(cnt_idx[:, s, :], key_i[:, bass.ds(c * CW, CW)]))
                    pool.sem_inc(idle, 1)
                    for j in range(CW):
                        indexed([], out=cnt_val[:, s, j:j + 1], out_offset=None, in_=key_count,
                                in_offset=at(cnt_idx[:, s, j:j + 1])).then_inc(cnt_got, 16)
                    pool.wait_ge(cnt_got, c * (16 * CW) + 16 * CW)
                    slow.link(gp.tensor_copy(total[:, bass.ds(c * CW, CW)], cnt_val[:, s, :]))
                even_chunks(pool, total_chunk, slow)
                pool.sem_inc(total_ready, 1)

            pool.wait_ge(pos_ready, 1)
            for j in range(R + TAIL):
                indexed([], out=sorted_rows, out_offset=at(padpos_i[:, j:j + 1]), in_=padrow[:, :], in_offset=None,
                        bounds_check=NT * P - 1, oob_is_err=False).then_inc(pads_out, 16)
            pool.wait_ge(inv_ready, 1)

            def place_chunk(c, i, s):
                wait(pool, sorted_out[s], i * (16 * CW))
                own.mark(gp.tensor_copy(pos_st[:, s, :], pos_i[:, bass.ds(c * CW, CW)]))
                own.mark(gp.tensor_copy(meta[:, s, :, D].bitcast(I32), src_i[:, bass.ds(c * CW, CW)]))
                own.mark(gp.tensor_copy(meta[:, s, :, D + 1], dst_f[:, bass.ds(c * CW, CW)]))
                own.link(gp.tensor_copy(meta[:, s, :, D + 2], inv[:, bass.ds(c * CW, CW)]))
                pool.sem_inc(idle, 1)
                for j in range(CW):
                    waits = [(attr_in[s], arrived(c, i, s))] if j == 0 else []
                    indexed(waits, out=sorted_rows, out_offset=at(pos_st[:, s, j:j + 1]), in_=meta[:, s, j, :],
                            in_offset=None, bounds_check=NT * P - 1, oob_is_err=False).then_inc(sorted_out[s], 16)
            chunks(pool, place_chunk, own)

            for l in range(L):
                def gather(i, k, j, l=l):
                    waits = []
                    s, q = k // 2, k % 2
                    if j == 0:
                        waits.append((xb_in[s][q], i * 16 + 16))
                        waits.append((t_ready, i * 4 + (k - 3)))
                    indexed([w for w in waits if not (isinstance(w[1], int) and w[1] <= 0)], out=hb[:, s, q * H + j, :],
                            out_offset=None, in_=h_tab[l],
                            in_offset=at(xb[:, s, q * H + j, D:D + 1].bitcast(U32))).then_inc(got[s][q], 16)

                def add(i, k, j, l=l):
                    s, q = k // 2, k % 2
                    waits = []
                    if j == 0:
                        waits.append((y_ready, i * 4 + (k + 1)))
                    waits.append((added[j % 2], (i * (2 * H) + (k * (H // 2) + j // 2)) * 16))
                    dma = indexed(waits, out=acc[l][j % 2], out_offset=at(idx_st[:, s, q * H + j:q * H + j + 1]),
                                  in_=yb[:, s, q * H + j, :], in_offset=None, compute_op=ALU.add)
                    dma.then_inc(added[j % 2], 16)
                    if j == 1:
                        pool.sem_inc(half_added, 1)

                if l == 0:
                    for s in range(2):
                        pool.wait_ge(h_out[s], 16 * plain_uses(s))
                else:
                    for s in range(2):
                        pool.wait_ge(sum_out[s], 16 * plain_uses(s))
                first_i = l * NG // 2
                for k in range(3):
                    for j in range(H):
                        gather(first_i, k, j)
                for s in range(2):
                    pool.wait_ge(o_out[s], 16 * plain_uses(s) * (l + 1))

                def turn(i, last, first_i=first_i):
                    for k in range(4):
                        for j in range(H):
                            if k == 0:
                                gather(i + first_i, 3, j)
                            elif not last:
                                gather(i + (first_i + 1), k - 1, j)
                            add(i + first_i, k, j)
                ends_loop(pool, NG // 2, turn)

        @block.vector
        def _(dve):
            v = nc.vector
            own = Chain(dve, dve_own)
            v.memset(zcol[:, :], 0.0)
            own.link(v.memset(ones[:, :], 1.0))
            v.memset(type_i[:, :], R)
            v.memset(src_i[:, :], 0)
            v.memset(near_i[:, :], -1)
            v.memset(dst_i[:, :], PADDST).then_inc(blank, 1)
            v.memset(zeros[:, :], 0.0).then_inc(blank, 1)
            v.memset(xc[:, :, :, :], 0.0)
            v.memset(meta[:, :, :, :], 0.0).then_inc(blank, 1)
            own.link(v.memset(padrow[:, :], 0.0))
            v.memset(padrow[:, D + 1:D + 2], float(PADDST))
            dve.wait_ge(consts, 5)
            v.tensor_copy(pidx[:, :], pidx_i[:, :])
            v.tensor_copy(tiota[:, :], tiota_i[:, :])
            dve.wait_ge(idx_in, 11 * 16)
            v.tensor_copy(dst_x[:, 0:1], near_i[:, 0:1])
            v.tensor_copy(dst_x[:, FE + 1:FE + 2], near_i[:, 1:2])
            v.tensor_copy(type_f[:, :], type_i[:, :])
            own.link(v.tensor_copy(dst_f, dst_i[:, :]))
            own.link(v.scalar_tensor_tensor(key[:, :], type_f[:, :], float(ROWS), dst_f, ALU.mult, ALU.add))
            own.mark(v.tensor_copy(key_i[:, :], key[:, :]))

            for r in range(R):
                own.link(v.tensor_scalar(eq[:, :], type_f[:, :], float(r), None, ALU.is_equal))
                own.link(v.tensor_tensor_scan(cum[:, r, :], eq[:, :], zcol[:, :], 0.0, ALU.add, ALU.add))
                own.link(v.tensor_copy(tot[:, r:r + 1], cum[:, r, FE - 1:FE]))
            dve.sem_inc(tot_ready, 1)
            dve.wait_ge(off_ready, 1)
            v.tensor_copy(off[:, :], ps_t[0][:, 0:R])
            own.link(v.tensor_copy(grand[:, :], ps_t[0][:, R:2 * R]))
            for l in range(L):
                last = v.tensor_copy(bias_b[:, l, :], ps_t[0][:, (l + 1) * D:(l + 2) * D])
            last.then_inc(off_read, 1)
            own.link(v.tensor_scalar(tmp[:, 0:R], grand[:, :], float(P - 1), None, ALU.add))
            own.link(v.tensor_copy(ntile_i[:, :], tmp[:, 0:R]))
            own.link(v.tensor_scalar(ntile_i[:, :], ntile_i[:, :], P.bit_length() - 1, None, ALU.arith_shift_right))
            own.link(v.tensor_copy(ntile[:, :], ntile_i[:, :]))
            own.link(v.tensor_tensor_scan(ends[:, :], ntile[:, :], zcol[:, 0:R], 0.0, ALU.add, ALU.add))
            own.link(v.tensor_tensor(base[:, :], ends[:, :], ntile[:, :], ALU.subtract))
            own.link(v.tensor_scalar(tile_type[:, :], tiota[:, :], base[0:1, 1:2], None, ALU.is_ge))
            for r in range(2, R):
                own.link(v.scalar_tensor_tensor(tile_type[:, :], tiota[:, :], base[0:1, r:r + 1], tile_type[:, :], ALU.is_ge, ALU.add))
            v.tensor_copy(tile_type_i[:, :], tile_type[:, :]).then_inc(types_ready, 1)
            own.link(v.tensor_scalar(base[:, :], base[:, :], float(P), None, ALU.mult))
            own.link(v.tensor_tensor(padpos[:, 0:R], base[:, :], grand[:, :], ALU.add))
            own.link(v.tensor_scalar(padpos[:, 0:R], padpos[:, 0:R], pidx[:, 0:1], None, ALU.add))
            own.link(v.scalar_tensor_tensor(padn[:, :], ntile[:, :], float(P), grand[:, :], ALU.mult, ALU.subtract))
            own.link(v.tensor_scalar(padn[:, :], padn[:, :], pidx[:, 0:1], BIG, ALU.is_le, ALU.mult))
            own.link(v.tensor_tensor(padpos[:, 0:R], padpos[:, 0:R], padn[:, :], ALU.add))
            own.link(v.tensor_scalar(tmp[:, 0:1], ends[:, R - 1:R], float(P), pidx[:, 0:1], ALU.mult, ALU.add))
            for j in range(TAIL):
                own.mark(v.tensor_scalar(padpos[:, R + j:R + j + 1], tmp[:, 0:1], float(j * P), None, ALU.add))
            dve.wait_ge(dve_own, own.count)
            own.mark(v.tensor_copy(padpos_i[:, :], padpos[:, :]))
            own.link(v.tensor_tensor(off[:, :], off[:, :], base[:, :], ALU.add))
            own.link(v.tensor_scalar(off[:, :], off[:, :], -1.0, None, ALU.add))
            own.link(v.tensor_scalar(pos[:, :], type_f[:, :], float(R), BIG, ALU.is_equal, ALU.mult))
            for r in range(R):
                own.link(v.tensor_scalar(eq[:, :], type_f[:, :], float(r), None, ALU.is_equal))
                own.link(v.scalar_tensor_tensor(tmp[:, :], cum[:, r, :], off[:, r:r + 1], eq[:, :], ALU.add, ALU.mult))
                own.link(v.tensor_tensor(pos[:, :], pos[:, :], tmp[:, :], ALU.add))
            v.tensor_copy(pos_i[:, :], pos[:, :]).then_inc(pos_ready, 1)

            own.link(v.tensor_tensor_reduce(out=tmp[:, :], in0=dst_x[:, 0:FE], in1=dst_f, scale=1.0, scalar=0.0,
                                            op0=ALU.subtract, op1=ALU.max, accum_out=falls[:, 0:1]))
            own.link(v.tensor_scalar(falls[:, :], falls[:, :], 0.0, None, ALU.is_gt))
            v.tensor_tensor(as_prev[:, :], dst_x[:, 0:FE], dst_f, ALU.is_equal)
            own.link(v.tensor_tensor(as_next[:, :], dst_x[:, 2:FE + 2], dst_f, ALU.is_equal))
            ways = ((as_prev[:, :], slice(None), FE - 1), (as_next[:, :], slice(None, None, -1), 0))

            def scan(out, keep, add, initial, way):
                return v.tensor_tensor_scan(out[:, way], keep[:, way], add[:, way], initial, ALU.mult, ALU.add)
            for w, (keep, way, end) in enumerate(ways):
                own.link(scan(run[:, :], keep, zcol[:, :], 1.0, way))
                own.link(v.tensor_copy(through[:, w:w + 1], run[:, end:end + 1]))
            for r in range(R):
                own.link(v.tensor_scalar(eq[:, :], type_f[:, :], float(r), None, ALU.is_equal))
                for w, (keep, way, end) in enumerate(ways):
                    own.link(scan(run[:, :], keep, eq[:, :], 0.0, way))
                    own.link(v.tensor_copy(tails[:, w, r:r + 1], run[:, end:end + 1]))
            own.link(v.memset(row_carry[:, :, :], 0.0))
            dve.sem_inc(tails_ready, 1)
            dve.wait_ge(rows_ps, 1)
            own.link(v.tensor_copy(row_in[:, :, :].rearrange("r k p -> r (k p)"), ps_t[1][0:R, :]))
            own.link(scan(row_carry[:, 0, 1:P + 1], row_in[:, 2, :], row_in[:, 0, :], 0.0, slice(None)))
            own.link(scan(row_carry[:, 1, 0:P], row_in[:, 3, :], row_in[:, 1, :], 0.0, slice(None, None, -1)))
            dve.sem_inc(carries_ready, 1)
            dve.wait_ge(carries_ps, 1)
            own.link(v.tensor_copy(carry_in[:, :, :].rearrange("p w r -> p (w r)"), ps_t[0][:, 0:2 * R]))
            v.tensor_scalar(flag_i[:, :], ps_t[0][0:1, 2 * R:2 * R + 1], 0.5, None, ALU.is_gt).then_inc(flag_ready, 1)
            own.link(v.memset(total[:, :], -1.0))
            for r in range(R):
                own.link(v.tensor_scalar(eq[:, :], type_f[:, :], float(r), None, ALU.is_equal))
                for w, (keep, way, end) in enumerate(ways):
                    own.link(scan(run[:, :], keep, eq[:, :], carry_in[:, w, r:r + 1], way))
                    own.link(v.tensor_tensor(tmp[:, :], run[:, :], eq[:, :], ALU.mult))
                    own.link(v.tensor_tensor(total[:, :], total[:, :], tmp[:, :], ALU.add))

            slow = Chain(dve, branch_own)
            dve.wait_ge(flag_ready, 1)
            unsorted = dve.value_load(flag_i[0:1, 0:1], min_val=0, max_val=1)
            with dve.If(unsorted > 0):
                def same_key(c, i, s):
                    v.tensor_copy(key_st[:, s, :], key[:, bass.ds(c * CW, CW)]).then_inc(kst_ready, 1)
                    for g, (a, w) in enumerate(groups_of(CW)):
                        dve.wait_ge(keyb_ready, c * NGR + (g + 1))
                        for j in range(w):
                            slow.link(v.tensor_scalar(same[:, j % 2, :], ps_t[g % 2][:, j * D:(j + 1) * D],
                                                     key_st[:, s, a + j:a + j + 1], None, ALU.is_equal))
                            ins = v.tensor_tensor_reduce(out=junk[:, :], in0=same[:, j % 2, :], in1=rank_w[:, :], scale=1.0,
                                                         scalar=0.0, op0=ALU.mult, op1=ALU.add,
                                                         accum_out=val_st[:, s, a + j:a + j + 1])
                            if j < w - 1:
                                slow.link(ins)
                            else:
                                slow.link(ins)
                                dve.sem_inc(keyb_read, 1)
                    slow.link(v.tensor_copy(in_tile[:, bass.ds(c * CW, CW)], val_st[:, s, :]))
                even_chunks(dve, same_key, slow)
                slow.link(v.tensor_scalar(eq[:, :], in_tile[:, :], float(2 * P), None, ALU.is_lt))
                slow.link(v.tensor_scalar(tmp[:, 0:1], pidx[:, 0:1], float(KEYS), None, ALU.add))
                slow.link(v.tensor_scalar(pos[:, :], key[:, :], tmp[:, 0:1], None, ALU.subtract))
                slow.link(v.tensor_tensor(pos[:, :], pos[:, :], eq[:, :], ALU.mult))
                slow.link(v.tensor_scalar(pos[:, :], pos[:, :], tmp[:, 0:1], None, ALU.add))
                v.tensor_copy(add_i[:, :], pos[:, :]).then_inc(cidx_ready, 1)
                dve.wait_ge(total_ready, 1)
            own.link(v.tensor_scalar(total[:, :], total[:, :], 1.0, None, ALU.max))
            v.reciprocal(inv[:, :], total[:, :]).then_inc(inv_ready, 1)

            def row_stats(c, i, s):
                dve.wait_ge(xc_in[s], arrived(c, i, s))
                for j in range(CW):
                    own.mark(v.bn_stats(st6[:, j, :], xc[:, s, j, :]))
                dve.wait_ge(dve_own, own.count)
                dve.sem_inc(dve_idle, 1)
                for j in range(CW):
                    own.mark(v.bn_aggr(mv[:, j, :], st6[:, j, :]))
                dve.wait_ge(dve_own, own.count)
                wait(dve, sd_ready, c)
                v.tensor_scalar(ve[:, :], mv[:, :, 1], LN_EPS, None, ALU.add).then_inc(ve_ready, 1)
                wait(dve, h_ready, c - 1)
                dve.wait_ge(sd_ready, c + 1)
                own.link(v.reciprocal(rstd[:, s, :], sd[:, :]))
                v.scalar_tensor_tensor(nmr[:, s, :], mv[:, :, 0], -1.0, rstd[:, s, :], ALU.mult, ALU.mult).then_inc(rs_ready, 1)

            def out_rows(c, s, l, n_stored):
                wait(dve, o_out[s], n_stored)
                k = c * NGR + l * NC * NGR
                for g, (a, w) in enumerate(groups_of(CW)):
                    dve.wait_ge(o_ps, k + (g + 1))
                    v.tensor_tensor(oc[:, s, a:a + w, :], ps_o[(s + g) % 2][:, 0:w * D].rearrange("p (w d) -> p w d", d=D),
                                    bias_b[:, l, :].unsqueeze(1).to_broadcast([P, w, D]), ALU.add).then_inc(o_ready, 1)

            def node_pass_0(c, i, s):
                row_stats(c, i, s)
                if isinstance(c, int) and c == 0:
                    return
                if s:
                    out_rows(c - 1, 0, 0, i * 16)
                else:
                    out_rows(c - 1, 1, 0, i * 16 - 16)
            chunks(dve, node_pass_0, own)
            out_rows(NC - 1, (NC - 1) % 2, 0, 16 * ((NC - 1) // 2))

            for l in range(L):
                def same_node(i, k, l=l):
                    s, q = k // 2, k % 2
                    hh = 4 * i + (k + l * 2 * NG)
                    bank = ps_t[q]
                    cols = slice(q * H, (q + 1) * H)
                    dve.wait_ge(d_ready, hh + 1)
                    wait(dve, ms_ready, hh - 1)
                    for j in range(H):
                        ins = v.tensor_scalar(sm[:, q, j * D:(j + 1) * D], bank[:, j * D:(j + 1) * D],
                                              xb[:, s, q * H + j, D + 1:D + 2], None, ALU.is_equal)
                        if l == 0:
                            own.mark(ins)
                        if j == H - 1:
                            if l == 0:
                                own.eng.wait_ge(own.sem, own.count)
                                dve.sem_inc(s_ready, 1)
                            else:
                                ins.then_inc(s_ready, 1)
                    if l == 0:
                        for j in range(H):
                            own.link(v.tensor_tensor_reduce(out=junk[:, :], in0=sm[:, q, j * D:(j + 1) * D], in1=rank_w[:, :],
                                                            scale=1.0, scalar=0.0, op0=ALU.mult, op1=ALU.add,
                                                            accum_out=rank_st[:, s, q * H + j:q * H + j + 1]))
                        own.link(v.tensor_scalar(first[:, :], rank_st[:, s, cols], float(2 * P), None, ALU.is_lt))
                        own.link(v.tensor_scalar(dsub[:, :], xb[:, s, cols, D + 1], repeat_row, None, ALU.subtract))
                        own.link(v.tensor_tensor(dsub[:, :], dsub[:, :], first[:, :], ALU.mult))
                        own.link(v.tensor_scalar(scat_idx[:, bass.ds(4 * H * i + k * H, H)], dsub[:, :], repeat_row, None, ALU.add))

                def edge_sum(i, k, l=l):
                    s, q = k // 2, k % 2
                    hh = 4 * i + (k + l * 2 * NG)
                    cols = slice(q * H, (q + 1) * H)
                    dve.wait_ge(got[s][q], (i + l * NG // 2) * (16 * H) + 16 * H)
                    wait(dve, m_ready, hh - 1)
                    h4 = hb[:, s, cols, :]
                    t4 = tb[:, q, :].rearrange("p (w d) -> p w d", d=D)
                    if l == 1:
                        own.link(v.tensor_tensor(h4, h4, bn_b[:, 0, 0, :].unsqueeze(1).to_broadcast([P, H, D]), ALU.mult))
                        own.link(v.tensor_tensor(h4, h4, bn_b[:, 0, 1, :].unsqueeze(1).to_broadcast([P, H, D]), ALU.add))
                        v.scalar_tensor_tensor(t4, h4, 0.0, xb[:, s, cols, 0:D], ALU.max, ALU.add).then_inc(t_ready, 1)
                    else:
                        v.tensor_tensor(t4, h4, xb[:, s, cols, 0:D], ALU.add).then_inc(t_ready, 1)

                def drain(i, k, l=l):
                    s, q = k // 2, k % 2
                    hh = 4 * i + (k + l * 2 * NG)
                    wait(dve, half_added, hh - 2)
                    dve.sem_inc(dve_idle, 1)
                    own.link(v.tensor_copy(idx_st[:, s, q * H:(q + 1) * H], scat_idx[:, bass.ds(4 * H * i + k * H, H)]))
                    dve.wait_ge(y_ps, hh + 1)
                    v.tensor_copy(yb[:, s, q * H:(q + 1) * H, :].rearrange("p w d -> p (w d)"), ps_y[q][:, :]).then_inc(y_ready, 1)

                if l == 0:
                    repeat_col = sb("repeat_col", [P, 1])
                    repeat_row = repeat_col[:, 0:1]
                    own.link(v.tensor_scalar(repeat_row, pidx[:, :], float(REPEAT), None, ALU.add))
                if l == 1:
                    def node_pass_1(c, i, s):
                        if isinstance(c, int) and c < 2:
                            stored = 16 * plain_uses(s)
                        else:
                            stored = i * 16 + 16 * plain_uses(s)
                        out_rows(c, s, 1, stored)
                    even_chunks(dve, node_pass_1, own)

                same_node(0, 0)

                def turn(i, last):
                    for k in range(4):
                        edge_sum(i, k)
                        if k < 3:
                            same_node(i, k + 1)
                        elif not last:
                            same_node(i + 1, 0)
                        drain(i, k)
                ends_loop(dve, NG // 2, turn, own)

                def table_sum(c, i, s, l=l):
                    dve.wait_ge(ab_in[s], i * 32 + (32 + 32 * plain_uses(s) * l))
                    if l == 0:
                        if isinstance(c, int) and c < 2:
                            dve.wait_ge(o_out[s], 16 * plain_uses(s))
                        wait(dve, sum_out[s], i * 16)
                    else:
                        if isinstance(c, int) and c < 2:
                            dve.wait_ge(o_out[s], 32 * plain_uses(s))
                        wait(dve, sum_out[s], i * 16 + 16 * plain_uses(s))
                    if not (isinstance(c, int) and c < 2 and l == 0):
                        dve.wait_ge(st_ps, (c - 1) * NGR + l * NC * NGR)
                    flat = "p c d -> p (c d)"
                    v.tensor_tensor(oc[:, s, :, :].rearrange(flat), xc[:, s, :, :].rearrange(flat),
                                    yc[:, s, :, :].rearrange(flat), ALU.add).then_inc(sum_ready, 1)
                    for g, (a, w) in enumerate(stat_groups(c)):
                        k = c * NGR + (l * NC * NGR + g + 1)
                        dve.wait_ge(st_ps, k)
                        n = P if a + w <= valid(c) else P - 1
                        v.bn_stats(bst[:, g % 2, :], ps_t[(s + g) % 2][:, 0:w * D].rearrange("p (w d) -> p w d", d=D)[:, :, 0:n]) \
                            .then_inc(st_read, 1)
                        dve.wait_ge(st_read, k)
                        own.mark(v.tensor_copy(bstat[:, bass.ds(c * NGR + g, 1), :].rearrange("p u k -> p (u k)"), bst[:, g % 2, :]))
                chunks(dve, table_sum, own)
                dve.wait_ge(dve_own, own.count)
                own.link(v.bn_aggr(bmv[:, :], bstat[:, 0:NC * NGR, :].rearrange("p n k -> p (n k)")))
                v.tensor_scalar(bsd[:, :], bmv[:, 1:2], BN_EPS, None, ALU.add).then_inc(bn_var, 1)
                dve.wait_ge(bn_sd, l + 1)
                own.link(v.reciprocal(brs[:, :], sd[:, 0:1]))
                own.link(v.tensor_tensor(bn_col[:, l, 0:1], brs[:, :], vec[:, 3 * l + 1:3 * l + 2], ALU.mult))
                own.link(v.tensor_tensor(tmp[:, 0:1], bmv[:, 0:1], bn_col[:, l, 0:1], ALU.mult))
                v.tensor_tensor(bn_col[:, l, 1:2], vec[:, 3 * l + 2:3 * l + 3], tmp[:, 0:1], ALU.subtract).then_inc(bn_ready, 1)
                dve.wait_ge(bnb_ps, l + 1)
                v.tensor_copy(bn_b[:, l, :, :].rearrange("p k d -> p (k d)"), ps_t[0][:, 0:2 * D]).then_inc(bnb_ready, 1)

            dve.wait_ge(bnb_ready, L)

            def final(c, i, s):
                if isinstance(c, int) and c < 2:
                    dve.wait_ge(sum_out[s], 32 * plain_uses(s))
                if not isinstance(c, int):
                    dve.wait_ge(f_in[s], i * 32 + 32)
                    dve.wait_ge(f_out[s], i * 16)
                else:
                    dve.wait_ge(f_in[s], arrived(c, i, s) + 16 * (c // 2 + 1))
                    wait(dve, f_out[s], arrived(c - 2, i, s) if c >= 2 else 0)
                x3, o3 = xc[:, s, :, :], oc[:, s, :, :]
                own.link(v.tensor_tensor(x3, x3, bn_b[:, 1, 0, :].unsqueeze(1).to_broadcast([P, CW, D]), ALU.mult))
                own.link(v.tensor_tensor(x3, x3, bn_b[:, 1, 1, :].unsqueeze(1).to_broadcast([P, CW, D]), ALU.add))
                v.tensor_tensor(o3, x3, yc[:, s, :, :], ALU.add).then_inc(f_ready, 1)
            chunks(dve, final, own)

        @block.scalar
        def _(act):
            a_ = nc.scalar
            act.wait_ge(blank, 3)
            for c in range(min(2, NC)):
                row_dma(act, xc[:, c % 2, :, :], x, c, xc_in[c % 2], True)

            def node_pass_0(c, i, s):
                act.wait_ge(ve_ready, c + 1)
                a_.activation(sd[:, :], ve[:, :], ACT.Sqrt).then_inc(sd_ready, 1)
                act.wait_ge(rs_ready, c + 1)
                wait(act, h_out[s], i * 16)
                if not isinstance(c, int) or c >= 2:
                    act.wait_ge(tr_ready, c * NGR - NGR)
                for j in range(CW):
                    ins = a_.activation(yc[:, s, j, :], xc[:, s, j, :], ACT.Relu, scale=rstd[:, s, j:j + 1], bias=nmr[:, s, j:j + 1])
                ins.then_inc(h_ready, 1)
                act.wait_ge(h_ready, c + 1)
                table_dma(act, yc[:, s, :, :], h_tab[0], c, h_out[s], False)
                if not isinstance(c, int) or c + 2 < NC:
                    row_dma(act, xc[:, s, :, :], x, c + 2, xc_in[s], True)
                if isinstance(c, int) and c == 0:
                    return
                turned(c - 1, 1 - s)
                if isinstance(c, int) and c == 1:
                    return
                act.wait_ge(o_ready, c * NGR - NGR)
                table_dma(act, oc[:, s, :, :], acc[0][0], c - 2, o_out[s], False)

            def turned(c, s):
                for g, (a, w) in enumerate(groups_of(CW)):
                    act.wait_ge(tr_ready, c * NGR + (g + 1))
                    a_.activation(ht[:, (s + g) % 2, 0:w * D], ps_t[(s + g) % 2][:, 0:w * D], ACT.Copy).then_inc(ht_ready, 1)

            def full_pairs(eng, body):
                pairs = max(0, (FULL - 2) // 2)

                def pair(i):
                    for s in range(2):
                        body(2 * i + s, i, s)
                pair_loop(eng, pairs, pair)
                for c in range(2 * pairs, NC):
                    body(c, c // 2, c % 2)
            full_pairs(act, node_pass_0)
            turned(NC - 1, (NC - 1) % 2)
            for c in (NC - 2, NC - 1):
                act.wait_ge(o_ready, (c + 1) * NGR)
                table_dma(act, oc[:, c % 2, :, :], acc[0][0], c, o_out[c % 2], False)

            for l in range(L):
                if l == 1:
                    act.wait_ge(bnb_ready, 1)
                    for s in range(2):
                        act.wait_ge(sum_out[s], 16 * plain_uses(s))

                    def load(c, s):
                        table_dma(act, xc[:, s, :, :], h_tab[1], c, xc_in[s], True)
                    for c in range(2):
                        load(c, c)

                    def node_pass_1(c, i, s):
                        for g, (a, w) in enumerate(groups_of(CW)):
                            act.wait_ge(tr_ready, c * NGR + (NC * NGR + g + 1))
                            if g == NGR - 1 and (not isinstance(c, int) or c + 2 < NC):
                                load(c + 2, s)
                            a_.activation(ht[:, (s + g) % 2, 0:w * D], ps_t[(s + g) % 2][:, 0:w * D], ACT.Relu,
                                          scale=bn_col[:, 0, 0:1], bias=bn_col[:, 0, 1:2]).then_inc(ht_ready, 1)
                        if isinstance(c, int) and c == 0:
                            return
                        act.wait_ge(o_ready, c * NGR + NC * NGR)
                        table_dma(act, oc[:, 1 - s, :, :], acc[1][0], c - 1, o_out[1 - s], False)
                    pairs = (NC - 2) // 2

                    def pair(i):
                        for s in range(2):
                            node_pass_1(2 * i + s, i, s)
                    pair_loop(act, pairs, pair)
                    for c in range(2 * pairs, NC):
                        node_pass_1(c, c // 2, c % 2)
                    act.wait_ge(o_ready, 2 * NC * NGR)
                    table_dma(act, oc[:, (NC - 1) % 2, :, :], acc[1][0], NC - 1, o_out[(NC - 1) % 2], False)

                def half(g, s, q):
                    hh = 2 * g + q
                    act.wait_ge(t_ready, hh + 1)
                    wait(act, ms_ready, hh - 1)
                    for j in range(H):
                        ins = a_.activation(mb[:, q, j * D:(j + 1) * D], tb[:, q, j * D:(j + 1) * D], ACT.Relu,
                                            scale=xb[:, s, q * H + j, D + 2:D + 3])
                    ins.then_inc(m_ready, 1)
                    act.wait_ge(ms_ready, hh + 1)
                    wait(act, y_ps, hh - 1)
                    a_.activation(mt[:, q, :], ps_m[q][:, :], ACT.Copy).then_inc(mt_ready, 1)

                def pair_e(i, l=l):
                    for s in range(2):
                        for q in range(2):
                            half(2 * i + (s + l * NG), s, q)
                pair_loop(act, NG // 2, pair_e)

                to = h_tab[1] if l == 0 else sum_rows

                def store(c, i, s, l=l, to=to):
                    act.wait_ge(sum_ready, c + (1 + l * NC))
                    table_dma(act, oc[:, s, :, :], to, c, sum_out[s], False)
                even_chunks(act, store)
                act.wait_ge(bn_var, l + 1)
                a_.activation(sd[:, 0:1], bsd[:, :], ACT.Sqrt).then_inc(bn_sd, 1)

            def final(c, i, s):
                act.wait_ge(f_ready, c + 1)
                row_dma(act, oc[:, s, :, :], out, c, f_out[s], False)
            chunks(act, final)

        @block.tensor
        def _(pe):
            te = nc.tensor

            def on_all(dst, col):
                return te.matmul(dst, col.to_broadcast([P, P]), ident[:, :], start=True, stop=True)

            pe.wait_ge(consts, 5)
            pe.wait_ge(params_in, 16 * 5 * L)
            pe.wait_ge(tot_ready, 1)
            te.matmul(ps_t[0][:, 0:R], before_p[:, :], tot[:, :], start=True, stop=True)
            te.matmul(ps_t[0][:, R:2 * R], ones[:, :], tot[:, :], start=True, stop=True)
            for l in range(L):
                last = on_all(ps_t[0][:, (l + 1) * D:(l + 2) * D], vec[:, 3 * l:3 * l + 1])
            last.then_inc(off_ready, 1)

            pe.wait_ge(tails_ready, 1)
            for w in range(2):
                te.matmul(ps_t[1][0:R, w * P:(w + 1) * P], tails[:, w, :], ident[:, :], start=True, stop=True)
                last = te.matmul(ps_t[1][0:R, (2 + w) * P:(3 + w) * P], through[:, w:w + 1].to_broadcast([P, R]), ident[:, :],
                                 start=True, stop=True)
            last.then_inc(rows_ps, 1)
            pe.wait_ge(off_read, 1)
            pe.wait_ge(carries_ready, 1)
            for w in range(2):
                te.matmul(ps_t[0][:, w * R:(w + 1) * R], row_carry[:, w, w:w + P], ident[0:R, 0:R], start=True, stop=True)
            te.matmul(ps_t[0][:, 2 * R:2 * R + 1], ones[:, :], falls[:, :], start=True, stop=True).then_inc(carries_ps, 1)
            pe.wait_ge(flag_ready, 1)
            unsorted = pe.value_load(flag_i[0:1, 0:1], min_val=0, max_val=1)

            with pe.If(unsorted > 0):
                def keys(c, i, s):
                    pe.wait_ge(kst_ready, c + 1)
                    for g, (a, w) in enumerate(groups_of(CW)):
                        k = c * NGR + g
                        if isinstance(c, int) and c == 0:
                            wait(pe, keyb_read, g - 1)
                        else:
                            pe.wait_ge(keyb_read, k if g == 0 else k - 1)
                        for j in range(w):
                            last = on_all(ps_t[g % 2][:, j * D:(j + 1) * D], key_st[:, s, a + j:a + j + 1])
                        last.then_inc(keyb_ready, 1)
                even_chunks(pe, keys)
                pe.wait_ge(keyb_read, NC * NGR)
            pe.wait_ge(types_ready, 1)

            def node_products(l, ready):
                def chunk(c, i, s):
                    ready(c, i, s)
                    source = (yc if l == 0 else xc)[:, s, :, :]
                    gs = groups_of(CW)

                    def turn(g):
                        a, w = gs[g]
                        for j in range(w):
                            last = te.transpose(ps_t[(s + g) % 2][:, j * D:(j + 1) * D], source[:, a + j, :], ident[:, :])
                        last.then_inc(tr_ready, 1)

                    def product(g):
                        a, w = gs[g]
                        k = c * NGR + (l * NC * NGR + g)
                        pe.wait_ge(ht_ready, k + 1)
                        wait(pe, o_ready, k - 1)
                        for j in range(w):
                            last = te.matmul(ps_o[(s + g) % 2][:, j * D:(j + 1) * D], ht[:, (s + g) % 2, j * D:(j + 1) * D],
                                             root_sb[:, l * D:(l + 1) * D], start=True, stop=True)
                        last.then_inc(o_ps, 1)
                    turn(0)
                    for g in range(1, NGR):
                        turn(g)
                        product(g - 1)
                    product(NGR - 1)
                return chunk

            chunks(pe, node_products(0, lambda c, i, s: pe.wait_ge(h_ready, c + 1)))

            for l in range(L):
                if l == 1:
                    def rows_in(c, i, s):
                        pe.wait_ge(xc_in[s], i * 16 + (16 + arrived(NC - 1 - (NC - 1 - s) % 2, 0, s)))
                    even_chunks(pe, node_products(1, rows_in))
                    pe.wait_ge(ht_ready, 2 * NC * NGR)

                def nodes_out(i, k, l=l):
                    s, q = k // 2, k % 2
                    hh = 4 * i + (k + l * 2 * NG)
                    pe.wait_ge(xb_in[s][q], (i + l * NG // 2) * 16 + 16)
                    wait(pe, s_ready, hh - 1)
                    for j in range(H):
                        last = on_all(ps_t[q][:, j * D:(j + 1) * D], xb[:, s, q * H + j, D + 1:D + 2])
                    last.then_inc(d_ready, 1)

                def products(i, k, l=l):
                    q = k % 2
                    hh = 4 * i + (k + l * 2 * NG)
                    kinds = [pe.value_load(tile_type_i[0:1, bass.ds(4 * H * i + (k * H + j), 1)], min_val=0, max_val=R - 1)
                             for j in range(H)]
                    pe.wait_ge(s_ready, hh + 1)
                    pe.wait_ge(m_ready, hh + 1)
                    wait(pe, mt_ready, hh - 1)
                    for j in range(H):
                        c = slice(j * D, (j + 1) * D)
                        last = te.matmul(ps_m[q][:, c], mb[:, q, c], sm[:, q, c], start=True, stop=True)
                    last.then_inc(ms_ready, 1)
                    pe.wait_ge(mt_ready, hh + 1)
                    wait(pe, y_ready, hh - 1)
                    for j in range(H):
                        c = slice(j * D, (j + 1) * D)
                        last = te.matmul(ps_y[q][:, c], mt[:, q, c], w_sb[l][:, bass.ds(kinds[j] * D, D)], start=True, stop=True)
                    last.then_inc(y_ps, 1)
                nodes_out(0, 0)

                def turn(i, last):
                    for k in range(4):
                        if k < 3:
                            nodes_out(i, k + 1)
                        elif not last:
                            nodes_out(i + 1, 0)
                        products(i, k)
                ends_loop(pe, NG // 2, turn)

                def feature_rows(c, i, s, l=l):
                    pe.wait_ge(sum_ready, c + (1 + l * NC))
                    for g, (a, w) in enumerate(stat_groups(c)):
                        if isinstance(c, int) and 2 * c + g < 2 and c == 0:
                            pass
                        else:
                            wait(pe, st_read, c * NGR + (g - 1 + l * NC * NGR))
                        for j in range(w):
                            last = te.transpose(ps_t[(s + g) % 2][:, j * D:(j + 1) * D], oc[:, s, a + j, :], ident[:, :])
                        last.then_inc(st_ps, 1)
                chunks(pe, feature_rows)
                pe.wait_ge(bn_ready, l + 1)
                for k in range(2):
                    last = on_all(ps_t[0][:, k * D:(k + 1) * D], bn_col[:, l, k:k + 1])
                last.then_inc(bnb_ps, 1)
                pe.wait_ge(bnb_ready, l + 1)


_INS = ['x', 'src', 'dst', 'edge_attr_128', 'edge_type_8', 'L0_gnn_weight', 'L0_gnn_root', 'L0_gnn_bias',
        'L0_gnn_bn_gamma', 'L0_gnn_bn_beta']


def kernel(**inputs):
    import numpy as _np
    import concourse.bacc as _bacc
    from concourse import mybir as _mybir
    from concourse.bass_utils import run_bass_kernel_spmd as _run

    nc = _bacc.Bacc("TRN2", target_bir_lowering=False, num_devices=1)
    arrays, args = {}, []
    for name in _INS:
        a = _np.ascontiguousarray(inputs[name])
        arrays[f"in_{name}_dram"] = a
        args.append(nc.dram_tensor(f"in_{name}_dram", a.shape, _mybir.dt.from_np(a.dtype), kind="ExternalInput").ap())
    out = nc.dram_tensor("out_0_dram", inputs["x"].shape, _mybir.dt.float32, kind="ExternalOutput").ap()
    gnn_kernel(nc, *args, out)
    r = _run(nc, [arrays], core_ids=[0])
    return r.results[0]["out_0_dram"]
```

```python
import math

import concourse.bass as bass
from concourse import mybir
from contextlib import ExitStack

P = 128
FP32 = mybir.dt.float32
I32 = mybir.dt.int32
U32 = mybir.dt.uint32
ALU = mybir.AluOpType
ACT = mybir.ActivationFunctionType
BN_EPS = 1e-5
LN_EPS = 1e-5
KEPT = 37


def wait(eng, sem, value):
    if isinstance(value, int) and value <= 0:
        return
    eng.wait_ge(sem, value)


class Chain:

    def __init__(self, eng, sem):
        self.eng, self.sem, self.count = eng, sem, 0

    def mark(self, instruction):
        instruction.then_inc(self.sem, 1)
        self.count = self.count + 1

    def link(self, instruction):
        self.mark(instruction)
        self.eng.wait_ge(self.sem, self.count)


def pair_loop(eng, pairs, body, chain=None):
    if not pairs:
        return
    before = chain.count if chain else 0
    body(0)
    step = chain.count - before if chain else 0
    if pairs > 1:
        with eng.Fori(1, pairs) as i:
            if chain:
                chain.count = i * step + before
            body(i)
        if chain:
            chain.count = before + step * pairs


def ends_loop(eng, turns, body, chain=None):
    pair_loop(eng, turns - 1, lambda i: body(i, False), chain)
    body(turns - 1, True)


def gnn_kernel(nc, x, src, dst, edge_attr, edge_type, weight, root, bias, gamma, beta, out):
    N, D = x.shape
    E = src.shape[0]
    L, R = weight.shape[0], weight.shape[1]
    assert D == P and edge_attr.shape == (E, D) and L == 2

    CW = 8
    F = -(-N // (P * CW)) * CW
    FE = F
    NC = F // CW
    PV = N - (P - 1) * F
    assert E == N and 0 < PV < F and PV % CW == 0
    FULL = PV // CW
    ROWS = P * (F + 2)
    REPEAT = P * F
    PADDST = P * (F + 1)
    G = 8
    H = 4
    NT = -(-((E + R * (P - 1)) // P) // (2 * G)) * 2 * G
    NG = NT // G
    TURNS = NG // 2
    ZH = -(-F // (4 * TURNS))
    Z = 4 * ZH
    assert F // Z >= TURNS - 1
    TAIL = NT - E // P
    M = D + 4
    ARENA = KEPT * CW * D
    KEEP = min(NC // 2, KEPT // 2) * 2
    KEYS = (R + 1) * ROWS
    BIG = float(1 << 22)

    def groups_of(cols):
        return [(a, min(H, cols - a)) for a in range(0, cols, H)]

    NGR = len(groups_of(CW))

    ctx = ExitStack()
    with ctx:
        def sb(name, shape, dt=FP32):
            return ctx.enter_context(nc.sbuf_tensor(name, shape, dt))

        def pb(name):
            return ctx.enter_context(nc.psum_tensor(name, [P, H * D], FP32))

        def sem(name):
            return ctx.enter_context(nc.semaphore(name))

        def dram(name, shape):
            return nc.dram_tensor(name, shape, FP32, kind="Internal").ap()

        h_tab = [dram("h0_rows", [P * F, D]), dram("h1_rows", [P * F, D])]
        acc = [[dram(f"acc_{l}_{k}", [ROWS, D]) for k in range(2)] for l in range(L)]
        sorted_rows = dram("sorted_rows", [NT * P, M])
        key_count = dram("key_count", [KEYS + P, 1])
        sum_rows = dram("sum_rows", [P * F, D])

        arena = sb("arena", [P, ARENA])
        early_end = 0

        def early(shape, dt=FP32):
            nonlocal early_end
            n = math.prod(shape[1:])
            flat = arena[:, early_end:early_end + n]
            early_end += n
            if dt != FP32:
                flat = flat.bitcast(dt)
            if len(shape) == 3:
                flat = flat.rearrange("p (a b) -> p a b", a=shape[1])
            if len(shape) == 4:
                flat = flat.rearrange("p (a b c) -> p a b c", a=shape[1], b=shape[2])
            return flat

        ident = sb("ident", [P, P])
        ones = sb("ones", [P, P])
        before_p = sb("before_p", [P, P])
        rank_w = sb("rank_w", [P, P])
        pidx = sb("pidx", [P, 1])
        pidx_i = sb("pidx_i", [P, 1], I32)
        zeros = early([P, Z * D])
        tiota_i = sb("tiota_i", [1, NT], I32)
        tiota = sb("tiota", [1, NT])
        w_sb = [early([P, R * D]) for l in range(L)]
        root_sb = sb("root_sb", [P, L * D])
        vec = sb("vec", [P, 6])
        bias_b = sb("bias_b", [P, L, D])
        bn_col = sb("bn_col", [P, L, 2])
        bn_b = sb("bn_b", [P, L, 2, D])

        type_i = early([P, FE], I32)
        src_i = early([P, FE], I32)
        dst_i = early([P, FE], I32)
        type_f = early([P, FE])
        dst_x = early([P, FE + 2])
        dst_f = dst_x[:, 1:FE + 1]
        near_i = sb("near_i", [P, 2], I32)
        as_prev = early([P, FE])
        as_next = early([P, FE])
        tails = sb("tails", [P, 2, R])
        through = sb("through", [P, 2])
        carry_in = sb("carry_in", [P, 2, R])
        row_in = sb("row_in", [R, 4, P])
        row_carry = sb("row_carry", [R, 2, P + 1])
        falls = sb("falls", [P, 1])
        flag_i = sb("flag_i", [1, 1], I32)
        run = early([P, FE])
        key = early([P, FE])
        key_i = early([P, FE], U32)
        add_i = early([P, FE], U32)
        in_tile = early([P, FE])
        total = early([P, FE])
        inv = early([P, FE])
        pos = early([P, FE])
        pos_i = early([P, FE], U32)
        cum = early([P, R, FE])
        eq = early([P, FE])
        tmp = early([P, FE])
        zcol = early([P, FE])
        tot = sb("tot", [P, R])
        off = sb("off", [P, R])
        grand = sb("grand", [P, R])
        ntile = sb("ntile", [P, R])
        ntile_i = sb("ntile_i", [P, R], I32)
        ends = sb("ends", [P, R])
        base = sb("base", [P, R])
        padn = sb("padn", [P, R])
        padpos = early([P, R + TAIL])
        padpos_i = early([P, R + TAIL], U32)
        padrow = early([P, M])
        tile_type = sb("tile_type", [1, NT])
        tile_type_i = sb("tile_type_i", [1, NT], I32)
        scat_idx = early([P, NT], U32)

        key_st = sb("key_st", [P, 2, CW])
        same = early([P, 2, D])
        junk = sb("junk", [P, D])
        val_st = sb("val_st", [P, 2, CW])
        cnt_idx = sb("cnt_idx", [P, 2, CW], U32)
        cnt_val = sb("cnt_val", [P, 2, CW])
        bias_rows = early([P, Z * D])
        meta = early([P, 2, CW, M])
        pos_st = sb("pos_st", [P, 2, CW], U32)
        xc = sb("xc", [P, 2, CW, D])
        yc = sb("yc", [P, 2, CW, D])
        oc = sb("oc", [P, 2, CW, D])
        hc = sb("hc", [P, 2, CW, D])
        st6 = sb("st6", [P, CW, 6])
        mv = sb("mv", [P, CW, 2])
        ve = sb("ve", [P, CW])
        sd = sb("sd", [P, CW])
        rstd = sb("rstd", [P, 2, CW])
        nmr = sb("nmr", [P, 2, CW])
        ht = sb("ht", [P, 2, H * D])
        xb = early([P, 2, G, M])
        hb = early([P, 2, G, D])
        sm = early([P, 2, H * D])
        tb = early([P, 2, H * D])
        mb = early([P, 2, H * D])
        mt = early([P, 2, H * D])
        yb = early([P, 2, G, D])
        rank_st = sb("rank_st", [P, 2, G])
        first = sb("first", [P, H])
        dsub = sb("dsub", [P, H])
        idx_st = sb("idx_st", [P, 2, G], U32)
        bstat = sb("bstat", [P, NC * NGR, 6])
        bst = sb("bst", [P, 2, 6])
        bmv = sb("bmv", [P, 2])
        bsd = sb("bsd", [P, 1])
        brs = sb("brs", [P, 1])
        mean_factor = sb("mean_factor", [P, 1])

        kept = arena[:, 0:KEEP * CW * D].rearrange("p (k n) -> p k n", k=KEEP)
        assert early_end <= ARENA

        ps_t = [pb("ps_t0"), pb("ps_t1")]
        ps_o = [pb("ps_o0"), pb("ps_o1")]
        ps_m = [pb("ps_m0"), pb("ps_m1")]
        ps_y = [pb("ps_y0"), pb("ps_y1")]

        consts = sem("consts")
        pool_own = sem("pool_own")
        dve_own = sem("dve_own")
        act_own = sem("act_own")
        dve_idle = sem("dve_idle")
        idle = sem("idle")
        sp_idle = sem("sp_idle")
        act_idle = sem("act_idle")
        params_in = sem("params_in")
        idx_in = sem("idx_in")
        blank = sem("blank")
        tot_ready = sem("tot_ready")
        off_ready = sem("off_ready")
        off_read = sem("off_read")
        bias_ps = sem("bias_ps")
        types_ready = sem("types_ready")
        pos_ready = sem("pos_ready")
        tables_zero = sem("tables_zero")
        counts_zero = sem("counts_zero")
        kst_ready = sem("kst_ready")
        keyb_ready = sem("keyb_ready")
        keyb_read = sem("keyb_read")
        cidx_ready = sem("cidx_ready")
        chain_sem = sem("chain_sem")
        cnt_got = sem("cnt_got")
        total_ready = sem("total_ready")
        tails_ready = sem("tails_ready")
        rows_ps = sem("rows_ps")
        carries_ready = sem("carries_ready")
        carries_ps = sem("carries_ps")
        flag_ready = sem("flag_ready")
        branch_own = sem("branch_own")
        pool_branch = sem("pool_branch")
        inv_ready = sem("inv_ready")
        attr_in = [sem("attr_in0"), sem("attr_in1")]
        sorted_out = [sem("sorted_out0"), sem("sorted_out1")]
        pads_out = sem("pads_out")
        xc_in = [sem("xc_in0"), sem("xc_in1")]
        ve_ready = sem("ve_ready")
        sd_ready = sem("sd_ready")
        rs_ready = sem("rs_ready")
        h_ready = sem("h_ready")
        h_out = [sem("h_out0"), sem("h_out1")]
        tr_ready = sem("tr_ready")
        ht_ready = sem("ht_ready")
        o_ps = sem("o_ps")
        o_ready = sem("o_ready")
        o_out = [sem("o_out0"), sem("o_out1")]
        xb_in = [[sem(f"xb_in{s}{q}") for q in range(2)] for s in range(2)]
        src_ready = sem("src_ready")
        got = [[sem(f"got{s}{q}") for q in range(2)] for s in range(2)]
        d_ready = sem("d_ready")
        s_ready = sem("s_ready")
        t_ready = sem("t_ready")
        m_ready = sem("m_ready")
        ms_ready = sem("ms_ready")
        mt_ready = sem("mt_ready")
        y_ps = sem("y_ps")
        y_ready = sem("y_ready")
        added = [sem("added0"), sem("added1")]
        half_added = sem("half_added")
        ab_in = [sem("ab_in0"), sem("ab_in1")]
        sum_ready = sem("sum_ready")
        sum_out = [sem("sum_out0"), sem("sum_out1")]
        st_ps = sem("st_ps")
        st_read = sem("st_read")
        bn_var = sem("bn_var")
        bn_sd = sem("bn_sd")
        bn_ready = sem("bn_ready")
        bnb_ps = sem("bnb_ps")
        bnb_ready = sem("bnb_ready")
        bias_ready = sem("bias_ready")
        tables_set = sem("tables_set")
        fa_in = [sem("fa_in0"), sem("fa_in1")]
        ab_ready = sem("ab_ready")
        hT_ps = sem("hT_ps")
        hT_ready = sem("hT_ready")
        own_ps = sem("own_ps")
        full_sum = sem("full_sum")
        sum_kept = sem("sum_kept")
        spill_out = [sem("spill_out0"), sem("spill_out1")]
        st2_ps = sem("st2_ps")
        st2_read = sem("st2_read")
        x_in = [sem("x_in0"), sem("x_in1")]
        spill_in = [sem("spill_in0"), sem("spill_in1")]
        xoff_ready = sem("xoff_ready")
        f_ready = sem("f_ready")
        f_out = [sem("f_out0"), sem("f_out1")]

        block = ctx.enter_context(nc.Block())

        def by_partition(a, rows):
            return bass.AP(a.tensor, 0, [[F * D, P], [1, rows * D]])

        def row_dma(eng, tile, a, c, rep, semaphore, load):
            n = P if rep < FULL else P - 1
            width = PV if rep < FULL else F
            far = bass.AP(a.tensor, 0, [[F * D, n], [1, width * D]])[:, bass.ds(c * (CW * D), CW * D)]
            far = far.rearrange("p (c d) -> p c d", d=D)
            for lo, hi in ((0, 112), (112, n)):
                o, i = (tile[lo:hi], far[lo:hi]) if load else (far[lo:hi], tile[lo:hi])
                eng.dma_start(o, i).then_inc(semaphore, 16)

        def table_dma(eng, tile, a, c, semaphore, load):
            far = by_partition(a, F)[:, bass.ds(c * (CW * D), CW * D)]
            near = tile.rearrange("p c d -> p (c d)")
            o, i = (near, far) if load else (far, near)
            eng.dma_start(o, i).then_inc(semaphore, 16)

        def chunks(eng, body, chain=None, cuts=()):
            marks = sorted({0, NC} | {k for k in cuts if 0 < k < NC})
            for a, b in zip(marks, marks[1:]):
                first, end = max(-(-a // 2) + 1, 2), b // 2
                if end <= first:
                    for c in range(a, b):
                        body(c, c // 2, c % 2, c)
                    continue
                for c in range(a, 2 * first):
                    if c == 2 * first - 2 and chain:
                        before = chain.count
                    body(c, c // 2, c % 2, c)
                if chain:
                    start = chain.count
                    step = start - before
                with eng.Fori(first, end) as i:
                    if chain:
                        chain.count = i * step + (start - first * step)
                    for s in range(2):
                        body(2 * i + s, i, s, 2 * first + s)
                if chain:
                    chain.count = start + step * (end - first)
                for c in range(2 * end, b):
                    body(c, c // 2, c % 2, c)

        def spilled(slot, a, b):
            return sum(1 for c in range(a, b) if c % 2 == slot)

        def plain_uses(slot):
            return (NC - slot + 1) // 2

        @block.sync
        def _(sp):
            sp.wait_ge(blank, 1)
            for near, far in ((type_i, edge_type), (dst_i, dst), (src_i, src)):
                for a, b in ((0, 112), (112, P - 1)):
                    sp.dma_start(near[a:b, :], bass.AP(far.tensor, a * FE, [[FE, b - a], [1, FE]])).then_inc(idx_in, 16)
                sp.dma_start(near[P - 1:P, 0:PV], bass.AP(far.tensor, (P - 1) * FE, [[FE, 1], [1, PV]])).then_inc(idx_in, 16)
            with nc.allow_non_contiguous_dma(reason="single columns, once"):
                sp.dma_start(near_i[1:P, 0:1], bass.AP(dst.tensor, FE - 1, [[FE, P - 1], [1, 1]])).then_inc(idx_in, 16)
                sp.dma_start(near_i[0:P - 1, 1:2], bass.AP(dst.tensor, FE, [[FE, P - 1], [1, 1]])).then_inc(idx_in, 16)
                for l in range(L):
                    for k, a in enumerate((bias, gamma, beta)):
                        sp.dma_start(vec[:, 3 * l + k:3 * l + k + 1], a[l, :].rearrange("(d u) -> d u", u=1)).then_inc(params_in, 16)
            for l in range(L):
                sp.dma_start(w_sb[l][:, :].rearrange("d (r o) -> d r o", r=R), weight[l].rearrange("r d o -> d r o")).then_inc(params_in, 16)
                sp.dma_start(root_sb[:, l * D:(l + 1) * D], root[l]).then_inc(params_in, 16)
            sp.wait_ge(blank, 2)
            n = (KEYS + P) // P
            flat = key_count.rearrange("(p c) u -> p (c u)", p=P)
            for a in range(0, n, Z * D):
                b = min(n, a + Z * D)
                sp.dma_start(flat[:, a:b], zeros[:, 0:b - a]).then_inc(counts_zero, 16)
            for l in range(L):
                for k in range(2):
                    sp.dma_start(acc[l][k][P * F:ROWS, :].rearrange("(p c) d -> p (c d)", p=P), zeros[:, 0:2 * D]).then_inc(tables_zero, 16)

            for c in range(NC):
                table_dma(sp, zeros[:, 0:CW * D].rearrange("p (c d) -> p c d", d=D), acc[0][1], c, tables_zero, False)

            sp.wait_ge(blank, 3)

            def attrs(c, i, s, rep):
                wait(sp, sorted_out[s], i * (16 * CW))
                sp.sem_inc(sp_idle, 1)
                row_dma(sp, meta[:, s, :, 0:D], edge_attr, c, rep, attr_in[s], True)
            chunks(sp, attrs, cuts=(FULL,))

            for l in range(L):
                if l == 0:
                    for s in range(2):
                        sp.wait_ge(sorted_out[s], 16 * CW * plain_uses(s))
                    sp.wait_ge(pads_out, 16 * (R + TAIL))
                    sp.wait_ge(bias_ready, 1)

                def rows(i, last, l=l):
                    for s in range(2):
                        for q in range(2):
                            hh = 4 * i + (2 * s + q + l * 2 * NG)
                            wait(sp, m_ready, hh - 3)
                            far = sorted_rows[bass.ds((4 * i + (2 * s + q)) * (H * P), H * P), :].rearrange("(g p) c -> p g c", p=P)
                            sp.dma_start(xb[:, s, q * H:(q + 1) * H, :], far).then_inc(xb_in[s][q], 16)
                            if l == 0:
                                a = (2 * s + q) * ZH
                                w = min(ZH, (F - (TURNS - 1) * Z if last else Z) - a)
                                for k, tile in enumerate((bias_rows, zeros)):
                                    if w > 0:
                                        sp.dma_start(by_partition(acc[1][k], F)[:, bass.ds((i * Z + a) * D, w * D)],
                                                     tile[:, 0:w * D]).then_inc(tables_set, 16)
                ends_loop(sp, TURNS, rows)

                for k in range(2):
                    sp.wait_ge(added[k], 16 * (l + 1) * NT // 2)

                if l == 0:
                    for s in range(2):
                        sp.wait_ge(h_out[s], 16 * plain_uses(s))
                    sp.wait_ge(o_ps, NC * NGR)

                    def ab(c, i, s, rep):
                        wait(sp, sum_ready, c - 1)
                        sp.sem_inc(sp_idle, 1)
                        table_dma(sp, xc[:, s, :, :], acc[0][0], c, ab_in[s], True)
                        table_dma(sp, yc[:, s, :, :], acc[0][1], c, ab_in[s], True)
                    chunks(sp, ab)

            for s in range(2):
                sp.wait_ge(sum_out[s], 16 * plain_uses(s))

            def last_sum(c, i, s, rep):
                wait(sp, ab_ready, c - 1)
                sp.sem_inc(sp_idle, 1)
                wait(sp, hT_ps, (c - 1) * NGR)
                sp.sem_inc(sp_idle, 1)
                table_dma(sp, xc[:, s, :, :], acc[1][0], c, fa_in[s], True)
                table_dma(sp, yc[:, s, :, :], acc[1][1], c, fa_in[s], True)
                table_dma(sp, hc[:, s, :, :], h_tab[1], c, fa_in[s], True)
            chunks(sp, last_sum)

            sp.wait_ge(ab_ready, NC)
            sp.wait_ge(hT_ps, NC * NGR)
            for s in range(2):
                wait(sp, spill_out[s], 16 * spilled(s, KEEP, NC))

            def final(c, i, s, rep):
                wait(sp, xoff_ready, c - 1)
                sp.sem_inc(sp_idle, 1)
                row_dma(sp, xc[:, s, :, :], x, c, rep, x_in[s], True)
                if rep >= KEEP:
                    wait(sp, f_ready, c - 1)
                    sp.sem_inc(sp_idle, 1)
                    table_dma(sp, hc[:, s, :, :], sum_rows, c, spill_in[s], True)
            chunks(sp, final, cuts=(KEEP, FULL))
            for s in range(2):
                sp.wait_ge(f_out[s], 32 * plain_uses(s))

        @block.gpsimd
        def _(pool):
            own = Chain(pool, pool_own)
            gp = nc.gpsimd
            own.link(gp.memset(ident[:, :], 0.0))
            gp.affine_select(out=ident[:, :], in_=ident[:, :], compare_op=ALU.not_equal, fill=1.0, base=0,
                             pattern=[[-1, P]], channel_multiplier=1).then_inc(consts, 1)
            own.link(gp.memset(before_p[:, :], 1.0))
            gp.affine_select(out=before_p[:, :], in_=before_p[:, :], compare_op=ALU.is_gt, fill=0.0, base=0,
                             pattern=[[1, P]], channel_multiplier=-1).then_inc(consts, 1)
            own.link(gp.memset(rank_w[:, :], float(2 * P + 1)))
            gp.affine_select(out=rank_w[:, :], in_=rank_w[:, :], compare_op=ALU.is_gt, fill=1.0, base=0,
                             pattern=[[-1, P]], channel_multiplier=1).then_inc(consts, 1)
            gp.iota(pidx_i[:, :], pattern=[[0, 1]], base=0, channel_multiplier=1).then_inc(consts, 1)
            gp.iota(tiota_i[:, :], pattern=[[1, NT]], base=0, channel_multiplier=0).then_inc(consts, 1)

            def indexed(reg_waits, **kw):
                for s, v in reg_waits:
                    if isinstance(v, int):
                        wait(pool, s, v)
                    else:
                        pool.wait_ge(s, v)
                        pool.sem_inc(idle, 1)
                return pool.indirect_dma_start(**kw)

            def at(ap):
                return bass.IndirectOffsetOnAxis(ap=ap, axis=0)

            slow = Chain(pool, pool_branch)
            pool.wait_ge(flag_ready, 1)
            unsorted = pool.value_load(flag_i[0:1, 0:1], min_val=0, max_val=1)
            with pool.If(unsorted > 0):
                pool.wait_ge(cidx_ready, 1)
                pool.wait_ge(counts_zero, 16 * -(-((KEYS + P) // P) // (Z * D)))

                def count_chunk(c, i, s, rep):
                    slow.mark(gp.tensor_copy(cnt_idx[:, s, :], add_i[:, bass.ds(c * CW, CW)]))
                    slow.link(gp.tensor_copy(cnt_val[:, s, :], in_tile[:, bass.ds(c * CW, CW)]))
                    pool.sem_inc(idle, 1)
                    for j in range(CW):
                        indexed([(chain_sem, c * (16 * CW) + 16 * j)], out=key_count, out_offset=at(cnt_idx[:, s, j:j + 1]),
                                in_=cnt_val[:, s, j:j + 1], in_offset=None, compute_op=ALU.add).then_inc(chain_sem, 16)
                chunks(pool, count_chunk, slow)
                pool.wait_ge(chain_sem, 16 * FE)

                def total_chunk(c, i, s, rep):
                    slow.link(gp.tensor_copy(cnt_idx[:, s, :], key_i[:, bass.ds(c * CW, CW)]))
                    pool.sem_inc(idle, 1)
                    for j in range(CW):
                        indexed([], out=cnt_val[:, s, j:j + 1], out_offset=None, in_=key_count,
                                in_offset=at(cnt_idx[:, s, j:j + 1])).then_inc(cnt_got, 16)
                    pool.wait_ge(cnt_got, c * (16 * CW) + 16 * CW)
                    slow.link(gp.tensor_copy(total[:, bass.ds(c * CW, CW)], cnt_val[:, s, :]))
                chunks(pool, total_chunk, slow)
                pool.sem_inc(total_ready, 1)

            pool.wait_ge(pos_ready, 1)
            for j in range(R + TAIL):
                indexed([], out=sorted_rows, out_offset=at(padpos_i[:, j:j + 1]), in_=padrow[:, :], in_offset=None,
                        bounds_check=NT * P - 1, oob_is_err=False).then_inc(pads_out, 16)
            pool.wait_ge(inv_ready, 1)

            def place_chunk(c, i, s, rep):
                wait(pool, sorted_out[s], i * (16 * CW))
                own.mark(gp.tensor_copy(pos_st[:, s, :], pos_i[:, bass.ds(c * CW, CW)]))
                own.mark(gp.tensor_copy(meta[:, s, :, D].bitcast(I32), src_i[:, bass.ds(c * CW, CW)]))
                own.mark(gp.tensor_copy(meta[:, s, :, D + 1], dst_f[:, bass.ds(c * CW, CW)]))
                own.link(gp.tensor_copy(meta[:, s, :, D + 2], inv[:, bass.ds(c * CW, CW)]))
                pool.sem_inc(idle, 1)
                for j in range(CW):
                    waits = [(attr_in[s], i * 32 + 32)] if j == 0 else []
                    indexed(waits, out=sorted_rows, out_offset=at(pos_st[:, s, j:j + 1]), in_=meta[:, s, j, :],
                            in_offset=None, bounds_check=NT * P - 1, oob_is_err=False).then_inc(sorted_out[s], 16)
            chunks(pool, place_chunk, own)

            for l in range(L):
                def gather(i, k, j, l=l):
                    waits = []
                    s, q = k // 2, k % 2
                    if j == 0:
                        waits.append((xb_in[s][q], i * 16 + 16))
                        waits.append((t_ready, i * 4 + (k - 3)))
                    indexed([w for w in waits if not (isinstance(w[1], int) and w[1] <= 0)], out=hb[:, s, q * H + j, :],
                            out_offset=None, in_=h_tab[l],
                            in_offset=at(xb[:, s, q * H + j, D:D + 1].bitcast(U32))).then_inc(got[s][q], 16)

                def add(i, k, j, l=l):
                    s, q = k // 2, k % 2
                    waits = []
                    if j == 0:
                        waits.append((y_ready, i * 4 + (k + 1)))
                    waits.append((added[j % 2], (i * (2 * H) + (k * (H // 2) + j // 2)) * 16))
                    dma = indexed(waits, out=acc[l][j % 2], out_offset=at(idx_st[:, s, q * H + j:q * H + j + 1]),
                                  in_=yb[:, s, q * H + j, :], in_offset=None, compute_op=ALU.add)
                    dma.then_inc(added[j % 2], 16)
                    if j == 1:
                        pool.sem_inc(half_added, 1)

                if l == 0:
                    for s in range(2):
                        pool.wait_ge(h_out[s], 16 * plain_uses(s))
                else:
                    for s in range(2):
                        pool.wait_ge(sum_out[s], 16 * plain_uses(s))
                first_i = l * NG // 2
                for k in range(3):
                    for j in range(H):
                        gather(first_i, k, j)
                if l == 0:
                    for s in range(2):
                        pool.wait_ge(o_out[s], 16 * plain_uses(s))
                    pool.wait_ge(tables_zero, 16 * (L * 2 + NC))
                else:
                    pool.wait_ge(tables_set, 16 * 2 * -(-F // ZH))

                def turn(i, last, first_i=first_i):
                    for k in range(4):
                        for j in range(H):
                            if k == 0:
                                gather(i + first_i, 3, j)
                            elif not last:
                                gather(i + (first_i + 1), k - 1, j)
                            add(i + first_i, k, j)
                ends_loop(pool, TURNS, turn)

            pool.wait_ge(bnb_ready, L)

            def x_and_offset(c, i, s, rep):
                pool.wait_ge(x_in[s], i * 32 + 32)
                wait(pool, f_ready, c - 1)
                pool.sem_inc(idle, 1)
                gp.tensor_tensor(yc[:, s, :, :], xc[:, s, :, :], bn_b[:, 1, 1, :].unsqueeze(1).to_broadcast([P, CW, D]),
                                 ALU.add).then_inc(xoff_ready, 1)
            chunks(pool, x_and_offset)

        @block.vector
        def _(dve):
            v = nc.vector
            own = Chain(dve, dve_own)
            v.memset(zcol[:, :], 0.0)
            own.link(v.memset(ones[:, :], 1.0))
            v.memset(type_i[:, :], R)
            v.memset(src_i[:, :], 0)
            v.memset(near_i[:, :], -1)
            v.memset(dst_i[:, :], PADDST).then_inc(blank, 1)
            v.memset(zeros[:, :], 0.0).then_inc(blank, 1)
            v.memset(xc[:, :, :, :], 0.0)
            v.memset(meta[:, :, :, :], 0.0).then_inc(blank, 1)
            own.link(v.memset(padrow[:, :], 0.0))
            v.memset(padrow[:, D + 1:D + 2], float(PADDST))
            dve.wait_ge(consts, 5)
            v.tensor_copy(pidx[:, :], pidx_i[:, :])
            v.tensor_copy(tiota[:, :], tiota_i[:, :])
            dve.wait_ge(idx_in, 11 * 16)
            v.tensor_copy(dst_x[:, 0:1], near_i[:, 0:1])
            v.tensor_copy(dst_x[:, FE + 1:FE + 2], near_i[:, 1:2])
            v.tensor_copy(type_f[:, :], type_i[:, :])
            own.link(v.tensor_copy(dst_f, dst_i[:, :]))
            own.link(v.scalar_tensor_tensor(key[:, :], type_f[:, :], float(ROWS), dst_f, ALU.mult, ALU.add))
            own.mark(v.tensor_copy(key_i[:, :], key[:, :]))

            for r in range(R):
                own.link(v.tensor_scalar(eq[:, :], type_f[:, :], float(r), None, ALU.is_equal))
                own.link(v.tensor_tensor_scan(cum[:, r, :], eq[:, :], zcol[:, :], 0.0, ALU.add, ALU.add))
                own.link(v.tensor_copy(tot[:, r:r + 1], cum[:, r, FE - 1:FE]))
            dve.sem_inc(tot_ready, 1)
            dve.wait_ge(off_ready, 1)
            v.tensor_copy(off[:, :], ps_t[0][:, 0:R])
            own.link(v.tensor_copy(grand[:, :], ps_t[0][:, R:2 * R]))
            for l in range(L):
                last = v.tensor_copy(bias_b[:, l, :], ps_t[0][:, (l + 1) * D:(l + 2) * D])
            last.then_inc(off_read, 1)
            own.link(v.tensor_scalar(tmp[:, 0:R], grand[:, :], float(P - 1), None, ALU.add))
            own.link(v.tensor_copy(ntile_i[:, :], tmp[:, 0:R]))
            own.link(v.tensor_scalar(ntile_i[:, :], ntile_i[:, :], P.bit_length() - 1, None, ALU.arith_shift_right))
            own.link(v.tensor_copy(ntile[:, :], ntile_i[:, :]))
            own.link(v.tensor_tensor_scan(ends[:, :], ntile[:, :], zcol[:, 0:R], 0.0, ALU.add, ALU.add))
            own.link(v.tensor_tensor(base[:, :], ends[:, :], ntile[:, :], ALU.subtract))
            own.link(v.tensor_scalar(tile_type[:, :], tiota[:, :], base[0:1, 1:2], None, ALU.is_ge))
            for r in range(2, R):
                own.link(v.scalar_tensor_tensor(tile_type[:, :], tiota[:, :], base[0:1, r:r + 1], tile_type[:, :], ALU.is_ge, ALU.add))
            v.tensor_copy(tile_type_i[:, :], tile_type[:, :]).then_inc(types_ready, 1)
            own.link(v.tensor_scalar(base[:, :], base[:, :], float(P), None, ALU.mult))
            own.link(v.tensor_tensor(padpos[:, 0:R], base[:, :], grand[:, :], ALU.add))
            own.link(v.tensor_scalar(padpos[:, 0:R], padpos[:, 0:R], pidx[:, 0:1], None, ALU.add))
            own.link(v.scalar_tensor_tensor(padn[:, :], ntile[:, :], float(P), grand[:, :], ALU.mult, ALU.subtract))
            own.link(v.tensor_scalar(padn[:, :], padn[:, :], pidx[:, 0:1], BIG, ALU.is_le, ALU.mult))
            own.link(v.tensor_tensor(padpos[:, 0:R], padpos[:, 0:R], padn[:, :], ALU.add))
            own.link(v.tensor_scalar(tmp[:, 0:1], ends[:, R - 1:R], float(P), pidx[:, 0:1], ALU.mult, ALU.add))
            for j in range(TAIL):
                own.mark(v.tensor_scalar(padpos[:, R + j:R + j + 1], tmp[:, 0:1], float(j * P), None, ALU.add))
            dve.wait_ge(dve_own, own.count)
            own.mark(v.tensor_copy(padpos_i[:, :], padpos[:, :]))
            own.link(v.tensor_tensor(off[:, :], off[:, :], base[:, :], ALU.add))
            own.link(v.tensor_scalar(off[:, :], off[:, :], -1.0, None, ALU.add))
            own.link(v.tensor_scalar(pos[:, :], type_f[:, :], float(R), BIG, ALU.is_equal, ALU.mult))
            for r in range(R):
                own.link(v.tensor_scalar(eq[:, :], type_f[:, :], float(r), None, ALU.is_equal))
                own.link(v.scalar_tensor_tensor(tmp[:, :], cum[:, r, :], off[:, r:r + 1], eq[:, :], ALU.add, ALU.mult))
                own.link(v.tensor_tensor(pos[:, :], pos[:, :], tmp[:, :], ALU.add))
            v.tensor_copy(pos_i[:, :], pos[:, :]).then_inc(pos_ready, 1)

            own.link(v.tensor_tensor_reduce(out=tmp[:, :], in0=dst_x[:, 0:FE], in1=dst_f, scale=1.0, scalar=0.0,
                                            op0=ALU.subtract, op1=ALU.max, accum_out=falls[:, 0:1]))
            own.link(v.tensor_scalar(falls[:, :], falls[:, :], 0.0, None, ALU.is_gt))
            v.tensor_tensor(as_prev[:, :], dst_x[:, 0:FE], dst_f, ALU.is_equal)
            own.link(v.tensor_tensor(as_next[:, :], dst_x[:, 2:FE + 2], dst_f, ALU.is_equal))
            ways = ((as_prev[:, :], slice(None), FE - 1), (as_next[:, :], slice(None, None, -1), 0))

            def scan(out, keep, add, initial, way):
                return v.tensor_tensor_scan(out[:, way], keep[:, way], add[:, way], initial, ALU.mult, ALU.add)
            for w, (keep, way, end) in enumerate(ways):
                own.link(scan(run[:, :], keep, zcol[:, :], 1.0, way))
                own.link(v.tensor_copy(through[:, w:w + 1], run[:, end:end + 1]))
            for r in range(R):
                own.link(v.tensor_scalar(eq[:, :], type_f[:, :], float(r), None, ALU.is_equal))
                for w, (keep, way, end) in enumerate(ways):
                    own.link(scan(run[:, :], keep, eq[:, :], 0.0, way))
                    own.link(v.tensor_copy(tails[:, w, r:r + 1], run[:, end:end + 1]))
            own.link(v.memset(row_carry[:, :, :], 0.0))
            dve.sem_inc(tails_ready, 1)
            dve.wait_ge(rows_ps, 1)
            own.link(v.tensor_copy(row_in[:, :, :].rearrange("r k p -> r (k p)"), ps_t[1][0:R, :]))
            own.link(scan(row_carry[:, 0, 1:P + 1], row_in[:, 2, :], row_in[:, 0, :], 0.0, slice(None)))
            own.link(scan(row_carry[:, 1, 0:P], row_in[:, 3, :], row_in[:, 1, :], 0.0, slice(None, None, -1)))
            dve.sem_inc(carries_ready, 1)
            dve.wait_ge(carries_ps, 1)
            own.link(v.tensor_copy(carry_in[:, :, :].rearrange("p w r -> p (w r)"), ps_t[0][:, 0:2 * R]))
            v.tensor_scalar(flag_i[:, :], ps_t[0][0:1, 2 * R:2 * R + 1], 0.5, None, ALU.is_gt).then_inc(flag_ready, 1)
            own.link(v.memset(total[:, :], -1.0))
            for r in range(R):
                own.link(v.tensor_scalar(eq[:, :], type_f[:, :], float(r), None, ALU.is_equal))
                for w, (keep, way, end) in enumerate(ways):
                    own.link(scan(run[:, :], keep, eq[:, :], carry_in[:, w, r:r + 1], way))
                    own.link(v.tensor_tensor(tmp[:, :], run[:, :], eq[:, :], ALU.mult))
                    own.link(v.tensor_tensor(total[:, :], total[:, :], tmp[:, :], ALU.add))

            slow = Chain(dve, branch_own)
            dve.wait_ge(flag_ready, 1)
            unsorted = dve.value_load(flag_i[0:1, 0:1], min_val=0, max_val=1)
            with dve.If(unsorted > 0):
                def same_key(c, i, s, rep):
                    v.tensor_copy(key_st[:, s, :], key[:, bass.ds(c * CW, CW)]).then_inc(kst_ready, 1)
                    for g, (a, w) in enumerate(groups_of(CW)):
                        dve.wait_ge(keyb_ready, c * NGR + (g + 1))
                        for j in range(w):
                            slow.link(v.tensor_scalar(same[:, j % 2, :], ps_t[g % 2][:, j * D:(j + 1) * D],
                                                     key_st[:, s, a + j:a + j + 1], None, ALU.is_equal))
                            ins = v.tensor_tensor_reduce(out=junk[:, :], in0=same[:, j % 2, :], in1=rank_w[:, :], scale=1.0,
                                                         scalar=0.0, op0=ALU.mult, op1=ALU.add,
                                                         accum_out=val_st[:, s, a + j:a + j + 1])
                            if j < w - 1:
                                slow.link(ins)
                            else:
                                slow.link(ins)
                                dve.sem_inc(keyb_read, 1)
                    slow.link(v.tensor_copy(in_tile[:, bass.ds(c * CW, CW)], val_st[:, s, :]))
                chunks(dve, same_key, slow)
                slow.link(v.tensor_scalar(eq[:, :], in_tile[:, :], float(2 * P), None, ALU.is_lt))
                slow.link(v.tensor_scalar(tmp[:, 0:1], pidx[:, 0:1], float(KEYS), None, ALU.add))
                slow.link(v.tensor_scalar(pos[:, :], key[:, :], tmp[:, 0:1], None, ALU.subtract))
                slow.link(v.tensor_tensor(pos[:, :], pos[:, :], eq[:, :], ALU.mult))
                slow.link(v.tensor_scalar(pos[:, :], pos[:, :], tmp[:, 0:1], None, ALU.add))
                v.tensor_copy(add_i[:, :], pos[:, :]).then_inc(cidx_ready, 1)
                dve.wait_ge(total_ready, 1)
            own.link(v.tensor_scalar(total[:, :], total[:, :], 1.0, None, ALU.max))
            v.reciprocal(inv[:, :], total[:, :]).then_inc(inv_ready, 1)

            own.mark(v.tensor_copy(bias_rows[:, :].rearrange("p (z d) -> p z d", d=D), bias_b[:, 1, :].unsqueeze(1).to_broadcast([P, Z, D])))
            dve.wait_ge(dve_own, own.count)
            dve.sem_inc(bias_ready, 1)

            def row_stats(c, i, s, rep):
                dve.wait_ge(xc_in[s], i * 32 + 32)
                for j in range(CW):
                    own.mark(v.bn_stats(st6[:, j, :], xc[:, s, j, :]))
                dve.wait_ge(dve_own, own.count)
                dve.sem_inc(dve_idle, 1)
                for j in range(CW):
                    own.mark(v.bn_aggr(mv[:, j, :], st6[:, j, :]))
                dve.wait_ge(dve_own, own.count)
                wait(dve, sd_ready, c)
                v.tensor_scalar(ve[:, :], mv[:, :, 1], LN_EPS, None, ALU.add).then_inc(ve_ready, 1)
                wait(dve, h_ready, c - 1)
                dve.wait_ge(sd_ready, c + 1)
                own.link(v.reciprocal(rstd[:, s, :], sd[:, :]))
                v.scalar_tensor_tensor(nmr[:, s, :], mv[:, :, 0], -1.0, rstd[:, s, :], ALU.mult, ALU.mult).then_inc(rs_ready, 1)

            def out_rows(c, i, s):
                wait(dve, o_out[s], i * 16)
                for g, (a, w) in enumerate(groups_of(CW)):
                    dve.wait_ge(o_ps, c * NGR + (g + 1))
                    v.tensor_tensor(oc[:, s, a:a + w, :], ps_o[g][:, 0:w * D].rearrange("p (w d) -> p w d", d=D),
                                    bias_b[:, 0, :].unsqueeze(1).to_broadcast([P, w, D]), ALU.add).then_inc(o_ready, 1)

            def node_pass(c, i, s, rep):
                row_stats(c, i, s, rep)
                if rep >= 2:
                    out_rows(c - 2, i - 1, s)
            chunks(dve, node_pass, own)
            for c in (NC - 2, NC - 1):
                out_rows(c, c // 2, c % 2)

            for l in range(L):
                def same_node(i, k, l=l):
                    s, q = k // 2, k % 2
                    hh = 4 * i + (k + l * 2 * NG)
                    bank = ps_t[q]
                    cols = slice(q * H, (q + 1) * H)
                    dve.wait_ge(d_ready, hh + 1)
                    wait(dve, ms_ready, hh - 1)
                    for j in range(H):
                        ins = v.tensor_scalar(sm[:, q, j * D:(j + 1) * D], bank[:, j * D:(j + 1) * D],
                                              xb[:, s, q * H + j, D + 1:D + 2], None, ALU.is_equal)
                        if l == 0:
                            own.mark(ins)
                        if j == H - 1:
                            if l == 0:
                                own.eng.wait_ge(own.sem, own.count)
                                dve.sem_inc(s_ready, 1)
                            else:
                                ins.then_inc(s_ready, 1)
                    if l == 0:
                        for j in range(H):
                            own.link(v.tensor_tensor_reduce(out=junk[:, :], in0=sm[:, q, j * D:(j + 1) * D], in1=rank_w[:, :],
                                                            scale=1.0, scalar=0.0, op0=ALU.mult, op1=ALU.add,
                                                            accum_out=rank_st[:, s, q * H + j:q * H + j + 1]))
                        own.link(v.tensor_scalar(first[:, :], rank_st[:, s, cols], float(2 * P), None, ALU.is_lt))
                        own.link(v.tensor_scalar(dsub[:, :], xb[:, s, cols, D + 1], repeat_row, None, ALU.subtract))
                        own.link(v.tensor_tensor(dsub[:, :], dsub[:, :], first[:, :], ALU.mult))
                        own.link(v.tensor_scalar(scat_idx[:, bass.ds(4 * H * i + k * H, H)], dsub[:, :], repeat_row, None, ALU.add))

                def edge_sum(i, k, l=l):
                    s, q = k // 2, k % 2
                    hh = 4 * i + (k + l * 2 * NG)
                    cols = slice(q * H, (q + 1) * H)
                    dve.wait_ge(got[s][q], (i + l * NG // 2) * (16 * H) + 16 * H)
                    wait(dve, m_ready, hh - 1)
                    h4 = hb[:, s, cols, :]
                    t4 = tb[:, q, :].rearrange("p (w d) -> p w d", d=D)
                    if l == 1:
                        own.link(v.tensor_tensor(h4, h4, bn_b[:, 0, 0, :].unsqueeze(1).to_broadcast([P, H, D]), ALU.mult))
                        own.link(v.tensor_tensor(h4, h4, bn_b[:, 0, 1, :].unsqueeze(1).to_broadcast([P, H, D]), ALU.add))
                        v.scalar_tensor_tensor(t4, h4, 0.0, xb[:, s, cols, 0:D], ALU.max, ALU.add).then_inc(t_ready, 1)
                    else:
                        v.tensor_tensor(t4, h4, xb[:, s, cols, 0:D], ALU.add).then_inc(t_ready, 1)

                def drain(i, k, l=l):
                    s, q = k // 2, k % 2
                    hh = 4 * i + (k + l * 2 * NG)
                    wait(dve, half_added, hh - 2)
                    dve.sem_inc(dve_idle, 1)
                    own.link(v.tensor_copy(idx_st[:, s, q * H:(q + 1) * H], scat_idx[:, bass.ds(4 * H * i + k * H, H)]))
                    dve.wait_ge(y_ps, hh + 1)
                    v.tensor_copy(yb[:, s, q * H:(q + 1) * H, :].rearrange("p w d -> p (w d)"), ps_y[q][:, :]).then_inc(y_ready, 1)

                if l == 0:
                    repeat_col = sb("repeat_col", [P, 1])
                    repeat_row = repeat_col[:, 0:1]
                    own.link(v.tensor_scalar(repeat_row, pidx[:, :], float(REPEAT), None, ALU.add))
                same_node(0, 0)
                edge_sum(0, 0)

                def turn(i, last):
                    for k in range(4):
                        ahead = (i, k + 1) if k < 3 else (i + 1, 0)
                        if k < 3 or not last:
                            same_node(*ahead)
                            edge_sum(*ahead)
                        drain(i, k)
                ends_loop(dve, TURNS, turn, own)

                def features(c, rep, bank, filled, read):
                    n = P if rep < FULL else P - 1
                    for g, (a, w) in enumerate(groups_of(CW)):
                        k = c * NGR + (g + 1)
                        dve.wait_ge(filled, k)
                        v.bn_stats(bst[:, g % 2, :], bank[g][:, 0:w * D].rearrange("p (w d) -> p w d", d=D)[:, :, 0:n]) \
                            .then_inc(read, 1)
                        dve.wait_ge(read, k)
                        own.mark(v.tensor_copy(bstat[:, bass.ds(c * NGR + g, 1), :].rearrange("p u k -> p (u k)"), bst[:, g % 2, :]))

                flat = "p c d -> p (c d)"
                if l == 0:
                    for s in range(2):
                        dve.wait_ge(o_out[s], 16 * plain_uses(s))

                    def table_sum(c, i, s, rep):
                        dve.wait_ge(ab_in[s], i * 32 + 32)
                        wait(dve, sum_out[s], i * 16)
                        wait(dve, st_ps, (c - 1) * NGR)
                        v.tensor_tensor(oc[:, s, :, :].rearrange(flat), xc[:, s, :, :].rearrange(flat),
                                        yc[:, s, :, :].rearrange(flat), ALU.add).then_inc(sum_ready, 1)
                        if rep >= 1:
                            features(c - 1, rep - 1, ps_t, st_ps, st_read)
                    chunks(dve, table_sum, own, cuts=(FULL + 1,))
                    features(NC - 1, NC - 1, ps_t, st_ps, st_read)
                else:
                    for s in range(2):
                        dve.wait_ge(sum_out[s], 16 * plain_uses(s))

                    def add_own(c, s):
                        for g, (a, w) in enumerate(groups_of(CW)):
                            dve.wait_ge(own_ps, c * NGR + (g + 1))
                            cols = oc[:, s, a:a + w, :].rearrange(flat)
                            ins = v.tensor_tensor(cols, cols, ps_o[g][:, 0:w * D], ALU.add)
                            ins.then_inc(full_sum, 1)

                    def table_sum(c, i, s, rep):
                        if rep >= 1:
                            dve.wait_ge(ab_ready, c)
                            add_own(c - 1, 1 - s)
                        dve.wait_ge(fa_in[s], i * 48 + 48)
                        if rep - 2 < KEEP:
                            wait(dve, sum_kept, c - 1)
                        else:
                            dve.wait_ge(spill_out[s], i * 16 - 16 * (KEEP // 2))
                        wait(dve, st2_ps, (c - 1) * NGR)
                        v.tensor_tensor(oc[:, s, :, :].rearrange(flat), xc[:, s, :, :].rearrange(flat),
                                        yc[:, s, :, :].rearrange(flat), ALU.add).then_inc(ab_ready, 1)
                        if rep >= 1:
                            features(c - 1, rep - 1, ps_m, st2_ps, st2_read)
                    chunks(dve, table_sum, own, cuts=(FULL + 1, KEEP + 2))
                    dve.wait_ge(ab_ready, NC)
                    add_own(NC - 1, (NC - 1) % 2)
                    features(NC - 1, NC - 1, ps_m, st2_ps, st2_read)
                dve.wait_ge(dve_own, own.count)
                own.link(v.bn_aggr(bmv[:, :], bstat[:, 0:NC * NGR, :].rearrange("p n k -> p (n k)")))
                v.tensor_scalar(bsd[:, :], bmv[:, 1:2], BN_EPS, None, ALU.add).then_inc(bn_var, 1)
                dve.wait_ge(bn_sd, l + 1)
                own.link(v.reciprocal(brs[:, :], sd[:, 0:1]))
                own.link(v.tensor_tensor(bn_col[:, l, 0:1], brs[:, :], vec[:, 3 * l + 1:3 * l + 2], ALU.mult))
                own.link(v.tensor_tensor(mean_factor[:, :], bmv[:, 0:1], bn_col[:, l, 0:1], ALU.mult))
                v.tensor_tensor(bn_col[:, l, 1:2], vec[:, 3 * l + 2:3 * l + 3], mean_factor[:, :], ALU.subtract).then_inc(bn_ready, 1)
                dve.wait_ge(bnb_ps, l + 1)
                v.tensor_copy(bn_b[:, l, :, :].rearrange("p k d -> p (k d)"), ps_t[0][:, 0:2 * D]).then_inc(bnb_ready, 1)

            dve.wait_ge(bnb_ready, L)
            dve.wait_ge(sum_kept, KEEP)

            def final(c, i, s, rep):
                if rep < KEEP:
                    sums = kept[:, bass.ds(c, 1), :].rearrange("p u (c d) -> p (u c) d", d=D)
                else:
                    dve.wait_ge(spill_in[s], i * 16 + (16 - 16 * (KEEP // 2)))
                    sums = hc[:, s, :, :]
                own.link(v.tensor_tensor(sums, sums, bn_b[:, 1, 0, :].unsqueeze(1).to_broadcast([P, CW, D]), ALU.mult))
                dve.wait_ge(xoff_ready, c + 1)
                wait(dve, f_out[s], i * 32)
                v.tensor_tensor(oc[:, s, :, :], sums, yc[:, s, :, :], ALU.add).then_inc(f_ready, 1)
            chunks(dve, final, own, cuts=(KEEP,))

        @block.scalar
        def _(act):
            a_ = nc.scalar
            act.wait_ge(blank, 3)
            for c in range(2):
                row_dma(act, xc[:, c, :, :], x, c, c, xc_in[c], True)

            def turned(c, rep):
                for g, (a, w) in enumerate(groups_of(CW)):
                    act.wait_ge(tr_ready, c * NGR + (g + 1))
                    if rep >= 1:
                        act.wait_ge(o_ps, c * NGR + (g + 1 - NGR))
                    a_.activation(ht[:, g, 0:w * D], ps_t[g][:, 0:w * D], ACT.Copy).then_inc(ht_ready, 1)

            def store_own(c, s):
                act.wait_ge(o_ready, c * NGR + NGR)
                table_dma(act, oc[:, s, :, :], acc[0][0], c, o_out[s], False)

            def node_pass(c, i, s, rep):
                act.wait_ge(ve_ready, c + 1)
                a_.activation(sd[:, :], ve[:, :], ACT.Sqrt).then_inc(sd_ready, 1)
                act.wait_ge(rs_ready, c + 1)
                wait(act, h_out[s], i * 16)
                if rep >= 2:
                    act.wait_ge(tr_ready, (c - 1) * NGR)
                for j in range(CW):
                    ins = a_.activation(yc[:, s, j, :], xc[:, s, j, :], ACT.Relu, scale=rstd[:, s, j:j + 1], bias=nmr[:, s, j:j + 1])
                ins.then_inc(h_ready, 1)
                act.wait_ge(h_ready, c + 1)
                table_dma(act, yc[:, s, :, :], h_tab[0], c, h_out[s], False)
                if rep + 2 < NC:
                    row_dma(act, xc[:, s, :, :], x, c + 2, rep + 2, xc_in[s], True)
                if rep >= 1:
                    turned(c - 1, rep - 1)
                if rep >= 2:
                    store_own(c - 2, s)
            chunks(act, node_pass, cuts=(FULL - 2, NC - 2))
            turned(NC - 1, NC - 1)
            for c in (NC - 2, NC - 1):
                store_own(c, c % 2)

            for l in range(L):
                def half(g, s, q):
                    hh = 2 * g + q
                    act.wait_ge(t_ready, hh + 1)
                    wait(act, ms_ready, hh - 1)
                    for j in range(H):
                        ins = a_.activation(mb[:, q, j * D:(j + 1) * D], tb[:, q, j * D:(j + 1) * D], ACT.Relu,
                                            scale=xb[:, s, q * H + j, D + 2:D + 3])
                    ins.then_inc(m_ready, 1)
                    act.wait_ge(ms_ready, hh + 1)
                    wait(act, y_ps, hh - 1)
                    a_.activation(mt[:, q, :], ps_m[q][:, :], ACT.Copy).then_inc(mt_ready, 1)

                def pair_e(i, l=l):
                    for s in range(2):
                        for q in range(2):
                            half(2 * i + (s + l * NG), s, q)
                pair_loop(act, TURNS, pair_e)

                if l == 0:
                    def store(c, i, s, rep):
                        act.wait_ge(sum_ready, c + 1)
                        table_dma(act, oc[:, s, :, :], h_tab[1], c, sum_out[s], False)
                    chunks(act, store)
                else:
                    def keep(c, s, rep):
                        act.wait_ge(full_sum, c * NGR + NGR)
                        if rep < KEEP:
                            a_.activation(kept[:, bass.ds(c, 1), :].rearrange("p u k -> p (u k)"),
                                          oc[:, s, :, :].rearrange("p c d -> p (c d)"), ACT.Copy).then_inc(sum_kept, 1)
                        else:
                            table_dma(act, oc[:, s, :, :], sum_rows, c, spill_out[s], False)

                    def own_part(c, i, s, rep):
                        for g, (a, w) in enumerate(groups_of(CW)):
                            act.wait_ge(hT_ps, c * NGR + (g + 1))
                            if rep >= 1:
                                act.wait_ge(own_ps, c * NGR + (g + 1 - NGR))
                            a_.activation(ht[:, g, 0:w * D], ps_t[g][:, 0:w * D], ACT.Relu,
                                          scale=bn_col[:, 0, 0:1], bias=bn_col[:, 0, 1:2]).then_inc(hT_ready, 1)
                        if rep >= 1:
                            keep(c - 1, 1 - s, rep - 1)
                    chunks(act, own_part, cuts=(KEEP + 1,))
                    keep(NC - 1, (NC - 1) % 2, NC - 1)
                act.wait_ge(bn_var, l + 1)
                a_.activation(sd[:, 0:1], bsd[:, :], ACT.Sqrt).then_inc(bn_sd, 1)

            def final(c, i, s, rep):
                act.wait_ge(f_ready, c + 1)
                row_dma(act, oc[:, s, :, :], out, c, rep, f_out[s], False)
            chunks(act, final, cuts=(FULL,))

        @block.tensor
        def _(pe):
            te = nc.tensor

            def on_all(dst, col):
                return te.matmul(dst, col.to_broadcast([P, P]), ident[:, :], start=True, stop=True)

            pe.wait_ge(consts, 5)
            pe.wait_ge(params_in, 16 * 5 * L)
            pe.wait_ge(tot_ready, 1)
            te.matmul(ps_t[0][:, 0:R], before_p[:, :], tot[:, :], start=True, stop=True)
            te.matmul(ps_t[0][:, R:2 * R], ones[:, :], tot[:, :], start=True, stop=True)
            for l in range(L):
                last = on_all(ps_t[0][:, (l + 1) * D:(l + 2) * D], vec[:, 3 * l:3 * l + 1])
            last.then_inc(off_ready, 1)

            pe.wait_ge(tails_ready, 1)
            for w in range(2):
                te.matmul(ps_t[1][0:R, w * P:(w + 1) * P], tails[:, w, :], ident[:, :], start=True, stop=True)
                last = te.matmul(ps_t[1][0:R, (2 + w) * P:(3 + w) * P], through[:, w:w + 1].to_broadcast([P, R]), ident[:, :],
                                 start=True, stop=True)
            last.then_inc(rows_ps, 1)
            pe.wait_ge(off_read, 1)
            pe.wait_ge(carries_ready, 1)
            for w in range(2):
                te.matmul(ps_t[0][:, w * R:(w + 1) * R], row_carry[:, w, w:w + P], ident[0:R, 0:R], start=True, stop=True)
            te.matmul(ps_t[0][:, 2 * R:2 * R + 1], ones[:, :], falls[:, :], start=True, stop=True).then_inc(carries_ps, 1)
            pe.wait_ge(flag_ready, 1)
            unsorted = pe.value_load(flag_i[0:1, 0:1], min_val=0, max_val=1)

            with pe.If(unsorted > 0):
                def keys(c, i, s, rep):
                    pe.wait_ge(kst_ready, c + 1)
                    for g, (a, w) in enumerate(groups_of(CW)):
                        k = c * NGR + g
                        if isinstance(c, int) and c == 0:
                            wait(pe, keyb_read, g - 1)
                        else:
                            pe.wait_ge(keyb_read, k if g == 0 else k - 1)
                        for j in range(w):
                            last = on_all(ps_t[g % 2][:, j * D:(j + 1) * D], key_st[:, s, a + j:a + j + 1])
                        last.then_inc(keyb_ready, 1)
                chunks(pe, keys)
                pe.wait_ge(keyb_read, NC * NGR)
            pe.wait_ge(types_ready, 1)

            def turn_chunk(source, bank, done, c, rep, emptied):
                for g, (a, w) in enumerate(groups_of(CW)):
                    if rep >= 1:
                        pe.wait_ge(emptied, c * NGR + (g + 1 - NGR))
                    for j in range(w):
                        last = te.transpose(bank[g][:, j * D:(j + 1) * D], source[:, a + j, :], ident[:, :])
                    last.then_inc(done, 1)

            def own_product(l, c, rep, ready, done, emptied):
                for g, (a, w) in enumerate(groups_of(CW)):
                    pe.wait_ge(ready, c * NGR + (g + 1))
                    if rep >= 1:
                        pe.wait_ge(emptied, c * NGR + (g + 1 - NGR))
                    for j in range(w):
                        last = te.matmul(ps_o[g][:, j * D:(j + 1) * D], ht[:, g, j * D:(j + 1) * D],
                                         root_sb[:, l * D:(l + 1) * D], start=True, stop=True)
                    last.then_inc(done, 1)

            def node_pass(c, i, s, rep):
                pe.wait_ge(h_ready, c + 1)
                turn_chunk(yc[:, s, :, :], ps_t, tr_ready, c, rep, ht_ready)
                if rep >= 1:
                    own_product(0, c - 1, rep - 1, ht_ready, o_ps, o_ready)
            chunks(pe, node_pass)
            own_product(0, NC - 1, NC - 1, ht_ready, o_ps, o_ready)

            for l in range(L):
                def nodes_out(i, k, l=l):
                    s, q = k // 2, k % 2
                    hh = 4 * i + (k + l * 2 * NG)
                    pe.wait_ge(xb_in[s][q], (i + l * NG // 2) * 16 + 16)
                    wait(pe, s_ready, hh - 1)
                    for j in range(H):
                        last = on_all(ps_t[q][:, j * D:(j + 1) * D], xb[:, s, q * H + j, D + 1:D + 2])
                    last.then_inc(d_ready, 1)

                def products(i, k, l=l):
                    q = k % 2
                    hh = 4 * i + (k + l * 2 * NG)
                    kinds = [pe.value_load(tile_type_i[0:1, bass.ds(4 * H * i + (k * H + j), 1)], min_val=0, max_val=R - 1)
                             for j in range(H)]
                    pe.wait_ge(s_ready, hh + 1)
                    pe.wait_ge(m_ready, hh + 1)
                    wait(pe, mt_ready, hh - 1)
                    for j in range(H):
                        c = slice(j * D, (j + 1) * D)
                        last = te.matmul(ps_m[q][:, c], mb[:, q, c], sm[:, q, c], start=True, stop=True)
                    last.then_inc(ms_ready, 1)
                    pe.wait_ge(mt_ready, hh + 1)
                    wait(pe, y_ready, hh - 1)
                    for j in range(H):
                        c = slice(j * D, (j + 1) * D)
                        last = te.matmul(ps_y[q][:, c], mt[:, q, c], w_sb[l][:, bass.ds(kinds[j] * D, D)], start=True, stop=True)
                    last.then_inc(y_ps, 1)
                nodes_out(0, 0)

                def turn(i, last):
                    for k in range(4):
                        if k < 3:
                            nodes_out(i, k + 1)
                        elif not last:
                            nodes_out(i + 1, 0)
                        products(i, k)
                ends_loop(pe, TURNS, turn)

                if l == 0:
                    def feature_rows(c, i, s, rep):
                        pe.wait_ge(sum_ready, c + 1)
                        turn_chunk(oc[:, s, :, :], ps_t, st_ps, c, rep, st_read)
                    chunks(pe, feature_rows)
                    pe.wait_ge(st_read, NC * NGR)
                else:
                    def last_sum(c, i, s, rep):
                        if rep >= 1:
                            own_product(1, c - 1, rep - 1, hT_ready, own_ps, full_sum)
                        pe.wait_ge(fa_in[s], i * 48 + 48)
                        turn_chunk(hc[:, s, :, :], ps_t, hT_ps, c, rep, hT_ready)
                        if rep >= 1:
                            pe.wait_ge(full_sum, c * NGR)
                            turn_chunk(oc[:, 1 - s, :, :], ps_m, st2_ps, c - 1, rep - 1, st2_read)
                    chunks(pe, last_sum)
                    own_product(1, NC - 1, NC - 1, hT_ready, own_ps, full_sum)
                    pe.wait_ge(full_sum, NC * NGR)
                    turn_chunk(oc[:, (NC - 1) % 2, :, :], ps_m, st2_ps, NC - 1, NC - 1, st2_read)
                    pe.wait_ge(hT_ready, NC * NGR)
                pe.wait_ge(bn_ready, l + 1)
                for k in range(2):
                    last = on_all(ps_t[0][:, k * D:(k + 1) * D], bn_col[:, l, k:k + 1])
                last.then_inc(bnb_ps, 1)
                pe.wait_ge(bnb_ready, l + 1)


_INS = ['x', 'src', 'dst', 'edge_attr_128', 'edge_type_8', 'L0_gnn_weight', 'L0_gnn_root', 'L0_gnn_bias',
        'L0_gnn_bn_gamma', 'L0_gnn_bn_beta']


def kernel(**inputs):
    import numpy as _np
    import concourse.bacc as _bacc
    from concourse import mybir as _mybir
    from concourse.bass_utils import run_bass_kernel_spmd as _run

    nc = _bacc.Bacc("TRN2", target_bir_lowering=False, num_devices=1)
    arrays, args = {}, []
    for name in _INS:
        a = _np.ascontiguousarray(inputs[name])
        arrays[f"in_{name}_dram"] = a
        args.append(nc.dram_tensor(f"in_{name}_dram", a.shape, _mybir.dt.from_np(a.dtype), kind="ExternalInput").ap())
    out = nc.dram_tensor("out_0_dram", inputs["x"].shape, _mybir.dt.float32, kind="ExternalOutput").ap()
    gnn_kernel(nc, *args, out)
    r = _run(nc, [arrays], core_ids=[0])
    return r.results[0]["out_0_dram"]
```
